# Optimizing a Trainium2 kernel written in Bass

```python
import numpy as np
import jax
import jax.numpy as jnp

def _softmax(x, axis=-1):
    return jax.nn.softmax(x, axis=axis)

def _gelu(x):
    return jax.nn.gelu(x, approximate=True)

def _silu(x):
    return jax.nn.silu(x)

def _sigmoid(x):
    return jax.nn.sigmoid(x)

def _layernorm(x, axis=-1, eps=1e-05):
    m = jnp.mean(x, axis=axis, keepdims=True)
    v = jnp.var(x, axis=axis, keepdims=True)
    return (x - m) / jnp.sqrt(v + eps)

def _scatter_add(tgt, idx, src, axis=0):
    return tgt.at[idx].add(src)

def _segment_sum(src, seg, n):
    return jax.ops.segment_sum(src, seg, n)
kernel_name = 'mk_gnn_resnorm_d2_gnn_r8_443f5c'

def setup_inputs(seed: int=0):
    np.random.seed(seed)
    _w = jnp.asarray

    def _rec_inputs():
        import jax
        import jax.numpy as jnp
        _gk = jax.random.key(seed)
        x = -0.000202 + 1 * jax.random.normal(jax.random.fold_in(_gk, 1), (12500, 128), jnp.float32)
        src = jax.random.randint(jax.random.fold_in(_gk, 2), (200000,), 0, 12500, jnp.int32)
        dst = jax.random.randint(jax.random.fold_in(_gk, 3), (200000,), 0, 12500, jnp.int32)
        _o = jnp.argsort(dst, stable=True)
        src = src[_o]
        dst = dst[_o]
        edge_attr_16 = 0.000254156 + 0.999948 * jax.random.normal(jax.random.fold_in(_gk, 11), (200000, 16), jnp.float32)
        edge_type_9 = jax.random.randint(jax.random.fold_in(_gk, 13), (200000,), 0, 9, jnp.int32)
        return (x, src, dst, edge_attr_16, edge_type_9)
    x, src, dst, edge_attr_16, edge_type_9 = _rec_inputs()

    def _L0_gnn_setup():
        import jax, jax.numpy as jnp
        import numpy as np
        NUM_EDGE_TYPES = 8
        HIDDEN = 128
        N_NODES = 6250
        N_EDGES = 75000

        def _gru_cell(x, h, W_ih, W_hh, b_ih, b_hh):
            H = h.shape[-1]
            gi = x @ W_ih.T + b_ih
            gh = h @ W_hh.T + b_hh
            i_r, i_z, i_n = (gi[:, :H], gi[:, H:2 * H], gi[:, 2 * H:])
            h_r, h_z, h_n = (gh[:, :H], gh[:, H:2 * H], gh[:, 2 * H:])
            r = jax.nn.sigmoid(i_r + h_r)
            z = jax.nn.sigmoid(i_z + h_z)
            n = jnp.tanh(i_n + r * h_n)
            return (1.0 - z) * n + z * h
        key = jax.random.key(seed)
        ks = jax.random.split(key, 10)
        H = HIDDEN
        h = jax.random.normal(ks[0], (N_NODES, H), dtype=jnp.float32)
        edge_index = jax.random.randint(ks[1], (2, N_EDGES), 0, N_NODES, dtype=jnp.int32)
        edge_type = jax.random.randint(ks[2], (N_EDGES,), 0, NUM_EDGE_TYPES + 1, dtype=jnp.int32)
        s = 1.0 / np.sqrt(H)
        W_msg = jax.random.uniform(ks[3], (H, H), jnp.float32, -s, s)
        b_msg = jax.random.uniform(ks[4], (H,), jnp.float32, -s, s)
        edge_embed = jax.random.normal(ks[5], (NUM_EDGE_TYPES + 1, H), dtype=jnp.float32)
        W_ih = jax.random.uniform(ks[6], (3 * H, H), jnp.float32, -s, s)
        W_hh = jax.random.uniform(ks[7], (3 * H, H), jnp.float32, -s, s)
        b_ih = jax.random.uniform(ks[8], (3 * H,), jnp.float32, -s, s)
        b_hh = jax.random.uniform(ks[9], (3 * H,), jnp.float32, -s, s)
        return {'h': h, 'edge_index': edge_index, 'edge_type': edge_type, 'num_nodes': N_NODES, 'W_msg': W_msg, 'b_msg': b_msg, 'edge_embed': edge_embed, 'W_ih': W_ih, 'W_hh': W_hh, 'b_ih': b_ih, 'b_hh': b_hh}
    _L0_gnn_all = _L0_gnn_setup()
    _L0_gnn_in = {k: v for k, v in _L0_gnn_all.items() if k in ('W_msg', 'b_msg', 'edge_embed', 'W_ih', 'W_hh', 'b_ih', 'b_hh')}
    del _L0_gnn_all

    def _L1_gnn_setup():
        import jax, jax.numpy as jnp
        import numpy as np
        N, E, H, DE = (6250, 100000, 128, 16)
        BN_EPS = 1e-05

        def _bn_eval(h, g, b, rm, rv):
            return g * (h - rm) * jax.lax.rsqrt(rv + BN_EPS) + b

        def _gin_layer(x, ei, ea, p, concat):
            enc_w, enc_b, w1, b1, g, be, rm, rv, w2, b2 = p
            ee = ea @ enc_w + enc_b
            src = x[ei[1]]
            h = jnp.concatenate([src, ee], axis=1) if concat else src + ee
            agg = jax.ops.segment_sum(h, ei[0], num_segments=x.shape[0])
            h = agg @ w1 + b1
            h = jax.nn.relu(_bn_eval(h, g, be, rm, rv))
            return h @ w2 + b2
        key = jax.random.key(seed)
        ks = jax.random.split(key, 32)
        d = {'x': jax.random.normal(ks[0], (N, H), jnp.float32), 'edge_index': jax.random.randint(ks[1], (2, E), 0, N, jnp.int64 if jax.config.jax_enable_x64 else jnp.int32), 'edge_attr': jax.random.normal(ks[2], (E, DE), jnp.float32), 'self_loop_index': 0, 'self_loop_type': 1, 'enc_w0': jax.random.normal(ks[3], (DE, H), jnp.float32) * 0.1, 'enc_b0': jax.random.normal(ks[4], (H,), jnp.float32) * 0.1, 'w1_0': jax.random.normal(ks[5], (H, 2 * H), jnp.float32) * 0.05, 'b1_0': jax.random.normal(ks[6], (2 * H,), jnp.float32) * 0.05, 'g0': jax.random.normal(ks[7], (2 * H,), jnp.float32), 'be0': jax.random.normal(ks[8], (2 * H,), jnp.float32) * 0.1, 'rm0': jax.random.normal(ks[9], (2 * H,), jnp.float32) * 0.1, 'rv0': jax.random.uniform(ks[10], (2 * H,), jnp.float32, 0.5, 1.5), 'w2_0': jax.random.normal(ks[11], (2 * H, H), jnp.float32) * 0.05, 'b2_0': jax.random.normal(ks[12], (H,), jnp.float32) * 0.05, 'enc_w': jax.random.normal(ks[13], (2, DE, H), jnp.float32) * 0.1, 'enc_b': jax.random.normal(ks[14], (2, H), jnp.float32) * 0.1, 'w1': jax.random.normal(ks[15], (2, 2 * H, 2 * H), jnp.float32) * 0.05, 'b1': jax.random.normal(ks[16], (2, 2 * H), jnp.float32) * 0.05, 'g': jax.random.normal(ks[17], (2, 2 * H), jnp.float32), 'be': jax.random.normal(ks[18], (2, 2 * H), jnp.float32) * 0.1, 'rm': jax.random.normal(ks[19], (2, 2 * H), jnp.float32) * 0.1, 'rv': jax.random.uniform(ks[20], (2, 2 * H), jnp.float32, 0.5, 1.5), 'w2': jax.random.normal(ks[21], (2, 2 * H, H), jnp.float32) * 0.05, 'b2': jax.random.normal(ks[22], (2, H), jnp.float32) * 0.05}
        return d
    _L1_gnn_all = _L1_gnn_setup()
    _L1_gnn_in = {k: v for k, v in _L1_gnn_all.items() if k in ('enc_w0', 'enc_b0', 'w1_0', 'b1_0', 'g0', 'be0', 'rm0', 'rv0', 'w2_0', 'b2_0', 'enc_w', 'enc_b', 'w1', 'b1', 'g', 'be', 'rm', 'rv', 'w2', 'b2')}
    del _L1_gnn_all
    return {'x': x, 'src': src, 'dst': dst, 'edge_attr_16': edge_attr_16, 'edge_type_9': edge_type_9, 'L0_gnn_W_msg': _L0_gnn_in['W_msg'], 'L0_gnn_b_msg': _L0_gnn_in['b_msg'], 'L0_gnn_edge_embed': _L0_gnn_in['edge_embed'], 'L0_gnn_W_ih': _L0_gnn_in['W_ih'], 'L0_gnn_W_hh': _L0_gnn_in['W_hh'], 'L0_gnn_b_ih': _L0_gnn_in['b_ih'], 'L0_gnn_b_hh': _L0_gnn_in['b_hh'], 'L1_gnn_enc_w0': _L1_gnn_in['enc_w0'], 'L1_gnn_enc_b0': _L1_gnn_in['enc_b0'], 'L1_gnn_w1_0': _L1_gnn_in['w1_0'], 'L1_gnn_b1_0': _L1_gnn_in['b1_0'], 'L1_gnn_g0': _L1_gnn_in['g0'], 'L1_gnn_be0': _L1_gnn_in['be0'], 'L1_gnn_rm0': _L1_gnn_in['rm0'], 'L1_gnn_rv0': _L1_gnn_in['rv0'], 'L1_gnn_w2_0': _L1_gnn_in['w2_0'], 'L1_gnn_b2_0': _L1_gnn_in['b2_0'], 'L1_gnn_enc_w': _L1_gnn_in['enc_w'], 'L1_gnn_enc_b': _L1_gnn_in['enc_b'], 'L1_gnn_w1': _L1_gnn_in['w1'], 'L1_gnn_b1': _L1_gnn_in['b1'], 'L1_gnn_g': _L1_gnn_in['g'], 'L1_gnn_be': _L1_gnn_in['be'], 'L1_gnn_rm': _L1_gnn_in['rm'], 'L1_gnn_rv': _L1_gnn_in['rv'], 'L1_gnn_w2': _L1_gnn_in['w2'], 'L1_gnn_b2': _L1_gnn_in['b2']}

def reference(x, src, dst, edge_attr_16, edge_type_9, L0_gnn_W_msg, L0_gnn_b_msg, L0_gnn_edge_embed, L0_gnn_W_ih, L0_gnn_W_hh, L0_gnn_b_ih, L0_gnn_b_hh, L1_gnn_enc_w0, L1_gnn_enc_b0, L1_gnn_w1_0, L1_gnn_b1_0, L1_gnn_g0, L1_gnn_be0, L1_gnn_rm0, L1_gnn_rv0, L1_gnn_w2_0, L1_gnn_b2_0, L1_gnn_enc_w, L1_gnn_enc_b, L1_gnn_w1, L1_gnn_b1, L1_gnn_g, L1_gnn_be, L1_gnn_rm, L1_gnn_rv, L1_gnn_w2, L1_gnn_b2):
    import jax
    import jax.numpy as jnp

    def _L0_gnn_ref(h, edge_index, edge_type, num_nodes, W_msg, b_msg, edge_embed, W_ih, W_hh, b_ih, b_hh):
        import jax, jax.numpy as jnp
        import numpy as np
        NUM_EDGE_TYPES = 8
        HIDDEN = 128
        N_NODES = 6250
        N_EDGES = 75000

        def _gru_cell(x, h, W_ih, W_hh, b_ih, b_hh):
            H = h.shape[-1]
            gi = x @ W_ih.T + b_ih
            gh = h @ W_hh.T + b_hh
            i_r, i_z, i_n = (gi[:, :H], gi[:, H:2 * H], gi[:, 2 * H:])
            h_r, h_z, h_n = (gh[:, :H], gh[:, H:2 * H], gh[:, 2 * H:])
            r = jax.nn.sigmoid(i_r + h_r)
            z = jax.nn.sigmoid(i_z + h_z)
            n = jnp.tanh(i_n + r * h_n)
            return (1.0 - z) * n + z * h
        src = edge_index[0]
        dst = edge_index[1]
        src_h = h[src] @ W_msg.T + b_msg
        emb = edge_embed[jnp.clip(edge_type, 0, NUM_EDGE_TYPES)]
        msg = src_h + emb
        messages = jax.ops.segment_sum(msg, dst, num_segments=num_nodes)
        h_new = _gru_cell(messages, h[:num_nodes], W_ih, W_hh, b_ih, b_hh)
        result = jnp.zeros_like(h).at[:num_nodes].set(h_new)
        return result

    def _L1_gnn_ref(x, edge_index, edge_attr, self_loop_index, self_loop_type, enc_w0, enc_b0, w1_0, b1_0, g0, be0, rm0, rv0, w2_0, b2_0, enc_w, enc_b, w1, b1, g, be, rm, rv, w2, b2):
        import jax, jax.numpy as jnp
        import numpy as np
        N, E, H, DE = (6250, 100000, 128, 16)
        BN_EPS = 1e-05

        def _bn_eval(h, g, b, rm, rv):
            return g * (h - rm) * jax.lax.rsqrt(rv + BN_EPS) + b

        def _gin_layer(x, ei, ea, p, concat):
            enc_w, enc_b, w1, b1, g, be, rm, rv, w2, b2 = p
            ee = ea @ enc_w + enc_b
            src = x[ei[1]]
            h = jnp.concatenate([src, ee], axis=1) if concat else src + ee
            agg = jax.ops.segment_sum(h, ei[0], num_segments=x.shape[0])
            h = agg @ w1 + b1
            h = jax.nn.relu(_bn_eval(h, g, be, rm, rv))
            return h @ w2 + b2
        n = x.shape[0]
        loops = jnp.arange(n, dtype=edge_index.dtype)
        ei = jnp.concatenate([edge_index, jnp.stack([loops, loops])], axis=1)
        sl_attr = jnp.zeros((n, edge_attr.shape[1]), edge_attr.dtype)
        sl_attr = sl_attr.at[:, self_loop_index].set(jnp.asarray(self_loop_type, edge_attr.dtype))
        ea = jnp.concatenate([edge_attr, sl_attr], axis=0)
        p0 = (enc_w0, enc_b0, w1_0, b1_0, g0, be0, rm0, rv0, w2_0, b2_0)
        h = jax.nn.relu(_gin_layer(x, ei, ea, p0, concat=False))
        for i in range(2):
            pi = tuple((a[i] for a in (enc_w, enc_b, w1, b1, g, be, rm, rv, w2, b2)))
            h = _gin_layer(h, ei, ea, pi, concat=True)
            if i < 1:
                h = jax.nn.relu(h)
        return h
    edge_index = jnp.stack([src, dst])
    x = _layernorm(x + _L0_gnn_ref(x, edge_index, edge_type_9, 12500, L0_gnn_W_msg, L0_gnn_b_msg, L0_gnn_edge_embed, L0_gnn_W_ih, L0_gnn_W_hh, L0_gnn_b_ih, L0_gnn_b_hh), axis=-1)
    x = _layernorm(x + _L1_gnn_ref(x, edge_index, edge_attr_16, 0, 1, L1_gnn_enc_w0, L1_gnn_enc_b0, L1_gnn_w1_0, L1_gnn_b1_0, L1_gnn_g0, L1_gnn_be0, L1_gnn_rm0, L1_gnn_rv0, L1_gnn_w2_0, L1_gnn_b2_0, L1_gnn_enc_w, L1_gnn_enc_b, L1_gnn_w1, L1_gnn_b1, L1_gnn_g, L1_gnn_be, L1_gnn_rm, L1_gnn_rv, L1_gnn_w2, L1_gnn_b2), axis=-1)
    return x

_drawn_inputs = setup_inputs


def setup_inputs(seed=0):
    import zlib

    import numpy as np

    out = dict(_drawn_inputs(seed))
    spreads = {}
    factors = {'L0_gnn_W_msg': 3.723,
     'L0_gnn_W_hh': 7.959,
     'L0_gnn_b_ih': 7.31,
     'L0_gnn_b_hh': 33.428,
     'L1_gnn_enc_w0': 3.347,
     'L1_gnn_b1_0': 6.456,
     'L1_gnn_be0': 3.437,
     'L1_gnn_rm0': 3.897,
     'L1_gnn_b2_0': 3.073,
     'L1_gnn_b1': 8.0,
     'L1_gnn_be': 8.0,
     'L1_gnn_rm': 7.074,
     'L1_gnn_b2': 8.0}
    for name, (base, spread) in spreads.items():
        noise = np.random.default_rng([zlib.crc32(name.encode()), seed]).standard_normal(out[name].shape)
        drawn = base * np.exp(spread * noise) if base else spread * noise
        out[name] = jnp.asarray(drawn.astype(out[name].dtype))
    for name, factor in factors.items():
        out[name] = (out[name] * factor).astype(out[name].dtype)
    return out
```

```python
import concourse.bass as bass
from concourse import mybir
from concourse.alu_op_type import AluOpType as ALU
from contextlib import ExitStack

F32 = mybir.dt.float32
BF16 = mybir.dt.bfloat16
I32 = mybir.dt.int32
ACT = mybir.ActivationFunctionType

P = 128
N = 12500
NB = 98
NP = NB * P
E = 200000
C = 1563
NT = C + NB
NTP = 1664
NBIN = NB + 1
W5 = 5
NG5 = 313
CH = 8
CW = CH * W5
NCH = (NG5 + CH - 1) // CH
RW = 20
EPS = 1e-5
GT = 4
NGR = (NT + GT - 1) // GT
RC = 64


class Queue:

    def __init__(self, ctx, nc, eng, name):
        self.ctx, self.nc, self.eng, self.name = ctx, nc, eng, name
        self.k, self.n, self.seen = 0, 0, {}
        self.sem = ctx.enter_context(nc.semaphore(f"{name}0"))

    def roll(self):
        self.k += 1
        self.n = 0
        self.sem = self.ctx.enter_context(self.nc.semaphore(f"{self.name}{self.k}"))

    def mark(self, ins):
        ins.then_inc(self.sem, 1)
        self.n += 1
        return (self.sem, self.n, f"{self.name}{self.k}")

    def done(self):
        if self.n:
            self.wait((self.sem, self.n, f"{self.name}{self.k}"))

    def wait(self, *marks):
        for m in marks:
            if m is not None and self.seen.get(m[2], 0) < m[1]:
                self.eng.wait_ge(m[0], m[1])
                self.seen[m[2]] = m[1]


class Lane:

    def __init__(self, ctx, nc, name):
        self.sem, self.n, self.name = ctx.enter_context(nc.semaphore(name)), 0, name

    def mark(self, ins):
        ins.then_inc(self.sem, 16)
        self.n += 16
        return (self.sem, self.n, self.name)


def program(nc, x, dst, src, typ, ea, wmsgT, wihT, whhT, emb, bmsg, bih, bhh, encT, w1a, w1b, w2, pv, out):
    ctx = ExitStack()
    with ctx:
        def sb(name, shape, dt=F32):
            return ctx.enter_context(nc.sbuf_tensor(name, shape, dt))

        def lane(name):
            return Lane(ctx, nc, name)

        DVE = Queue(ctx, nc, nc.vector, "dve")
        ACE = Queue(ctx, nc, nc.scalar, "act")
        PE = Queue(ctx, nc, nc.tensor, "pe")
        POOL = Queue(ctx, nc, nc.gpsimd, "pool")
        SP = Queue(ctx, nc, nc.sync, "sp")
        v, s, t, g = nc.vector, nc.scalar, nc.tensor, nc.gpsimd

        RBd = nc.dram_tensor("rec_b", (P * NTP, 3), F32).ap()
        RAd = nc.dram_tensor("rec_a", (P * NTP, RW), F32).ap()
        X1d = nc.dram_tensor("x1_rows", (NP, P), F32).ap()
        H1d = nc.dram_tensor("h1_rows", (NP, P), F32).ap()
        H2d = nc.dram_tensor("h2_rows", (NP, P), F32).ap()

        BIG = sb("BIG", [P, 2 * NP])
        XR = sb("XR", [P, 6800])
        DR = sb("DR", [P, 7600])
        BT = sb("BT", [33, NTP], I32)
        G = sb("G", [P, 4, GT, P])
        S = sb("S", [P, 4, GT, P])
        WM = sb("WM", [P, P])
        WI = sb("WI", [P, 384])
        WH = sb("WH", [P, 384])
        EC = sb("EC", [P, 51])
        W1A = sb("W1A", [P, 3, 256])
        W1B = sb("W1B", [P, 2, 256])
        W2 = sb("W2", [P, 3, 2, P])
        MM = sb("MM", [17, 3, 256])
        EB = sb("EB", [64, 2, P])
        PV = sb("PV", [P, 33])
        SCL = sb("SCL", [P, 3, 4])
        BR = sb("BR", [1, 3, 512])
        IOTA = sb("IOTA", [P, P])
        DIF = sb("DIF", [P, P])
        TRI = sb("TRI", [P, P])
        IDN = sb("IDN", [P, P])
        IDB = sb("IDB", [P, P], BF16)
        ONE = sb("ONE", [P, P])
        ONB = sb("ONB", [P, 1], BF16)
        V17 = sb("V17", [17, 4])
        CNT = sb("CNT", [P, 2, NBIN])
        BASE = sb("BASE", [P, 2, NBIN])
        SM = sb("SM", [P, 4, 100])
        SMI = sb("SMI", [P, 2, 100], I32)
        SC = sb("SC", [P, 4, 4])
        SCI = sb("SCI", [P, 2, 4], I32)
        EP = sb("EP", [P, 1])

        AGG = BIG[:, 0:NP]
        T9 = BIG[32:41, NP:2 * NP]
        T17 = BIG[0:17, NP:2 * NP]

        def carve(base):
            at = [0]

            def take(words):
                a = at[0]
                at[0] += words
                return base[:, a:a + words]
            return take

        lo = carve(BIG[:, 0:NP])
        TYPi = lo(C).bitcast(I32)
        SRCi = lo(C).bitcast(I32)
        HI = [lo(788).bitcast(BF16) for _ in range(2)]
        JUNK = [lo(788).bitcast(BF16) for _ in range(2)]
        TMPI = lo(C).bitcast(I32)
        OH = [lo(248).bitcast(BF16)[:, 0:W5 * NBIN].rearrange("p (c b) -> p c b", b=NBIN) for _ in range(4)]
        PRD = [lo(W5 * NBIN).rearrange("p (c b) -> p c b", b=NBIN) for _ in range(2)]
        RNK = [lo(CW) for _ in range(2)]
        RKI = [lo(3 * CW).bitcast(I32).rearrange("p (a c) -> p a c", a=3) for _ in range(2)]
        hi_ = carve(BIG[:, NP:2 * NP])
        RECB = hi_(3 * C).rearrange("p (c w) -> p c w", w=3)
        POSB = hi_(C).bitcast(I32)
        NULA = hi_(52 * RW).rearrange("p (c w) -> p c w", w=RW)
        NULB = hi_(416 * 3).rearrange("p (c w) -> p c w", w=3)
        IOTT = hi_(NTP)
        GE = hi_(NTP // 2).bitcast(BF16)
        xr = carve(XR)
        POSA = xr(C).bitcast(I32)
        DSTi = xr(C).bitcast(I32)
        RELS = xr(782).bitcast(BF16)
        EAR = [xr(CW * 16).rearrange("p (c w) -> p c w", w=16) for _ in range(2)]
        RECA = [xr(CW * RW).rearrange("p (c w) -> p c w", w=RW) for _ in range(2)]
        xr2 = carve(XR)
        RAR = [xr2(RC * RW).rearrange("p (c w) -> p c w", w=RW) for _ in range(3)]
        IDXA = xr2(NTP).bitcast(I32)
        RELA = xr2(NTP // 2).bitcast(BF16)
        dr0 = carve(DR)
        RBs = dr0(NTP * 3).rearrange("p (c w) -> p c w", w=3)
        OT = [dr0(GT * 9).rearrange("p (c w) -> p c w", w=9) for _ in range(4)]
        dr = carve(DR)
        XB = [dr(P) for _ in range(4)]
        XMT = [dr(2 * P) for _ in range(2)]
        RZ = [dr(2 * P) for _ in range(2)]
        TN = [dr(P) for _ in range(2)]
        DD = [dr(2 * P) for _ in range(2)]
        Y = [dr(14 * P).rearrange("p (c w) -> p c w", w=P) for _ in range(2)]
        ST = [dr(14 * 8).rearrange("p (c w) -> p c w", w=8) for _ in range(2)]
        dr2 = carve(DR)
        HID = [dr2(1024).rearrange("p (c w) -> p c w", w=512) for _ in range(2)]
        TRS = [dr2(512).rearrange("p (c w) -> p c w", w=P) for _ in range(2)]
        XO = [dr2(512).rearrange("p (c w) -> p c w", w=P) for _ in range(2)]
        ST2 = [dr2(32).rearrange("p (c w) -> p c w", w=8) for _ in range(2)]
        OUTS = [dr2(512) for _ in range(2)]

        PS = [ctx.enter_context(nc.psum_tensor(f"ps{i}", [P, 512], F32)) for i in range(8)]

        l_idx = lane("l_idx")
        for to, frm in ((DSTi, dst), (SRCi, src), (TYPi, typ)):
            got_idx = l_idx.mark(nc.sync.dma_start(to, frm))
        l_w = lane("l_w")
        for to, frm in ((WM[:], wmsgT), (WI[:], wihT), (WH[:], whhT), (EC[:], encT),
                        (W1A[:], w1a.rearrange("p (i n) -> p i n", i=3)),
                        (W1B[:], w1b.rearrange("p (i n) -> p i n", i=2)),
                        (W2[:], w2.rearrange("p (i k n) -> p i k n", i=3, k=2)), (PV[:], pv),
                        (EB[32:41, 0, :], emb), (EB[32:41, 1, :], bmsg.broadcast_to([9, P])),
                        (BR[0:1, 0, 0:384], bih), (BR[0:1, 1, 0:384], bhh)):
            got_w = l_w.mark(nc.sync.dma_start(to, frm))

        POOL.mark(g.iota(IOTA[:], [[1, P]], base=0, channel_multiplier=0, allow_small_or_imprecise_dtypes=True))
        POOL.mark(g.iota(DIF[:], [[1, P]], base=0, channel_multiplier=-1, allow_small_or_imprecise_dtypes=True))
        m_iota = POOL.mark(g.iota(IOTT, [[1, NTP]], base=0, channel_multiplier=0,
                                  allow_small_or_imprecise_dtypes=True))
        DVE.mark(v.memset(ONE[:], 1.0))
        DVE.mark(v.memset(EP[:], EPS))
        DVE.mark(v.memset(ONB[:], 1.0))
        m0 = DVE.mark(v.memset(NULB[:, :, :], 0.0))
        DVE.wait(m0)
        m_nb = DVE.mark(v.memset(NULB[:, :, 1:2], -1.0))
        m0 = DVE.mark(v.memset(NULA[:, :, :], 0.0))
        DVE.wait(m0)
        m_na = DVE.mark(v.memset(NULA[:, :, 1:2], -1.0))
        DVE.wait(m_iota)
        DVE.mark(v.tensor_scalar(TRI[:], DIF[:], 0.0, None, ALU.is_gt))
        DVE.mark(v.tensor_scalar(IDN[:], DIF[:], 0.0, None, ALU.is_equal))
        m_c = DVE.mark(v.tensor_scalar(IDB[:], DIF[:], 0.0, None, ALU.is_equal))
        SP.wait(m_nb)
        l_nb, l_na = lane("l_nb"), lane("l_na")
        RBv = RBd.rearrange("(p c) w -> p c w", p=P)
        RAv = RAd.rearrange("(p c) w -> p c w", p=P)
        for i in range(4):
            null_b = l_nb.mark(nc.sync.dma_start(RBv[:, 416 * i:416 * (i + 1), :], NULB))
        SP.wait(m_na)
        for i in range(32):
            null_a = l_na.mark(nc.sync.dma_start(RAv[:, 52 * i:52 * (i + 1), :], NULA))

        def sort(d, SEG, place, ready):
            DVE.wait(got_idx)
            DVE.done()
            m = DVE.mark(v.tensor_scalar(TMPI, SEG, 7, None, ALU.logical_shift_right))
            m1 = DVE.mark(v.memset(HI[d][:, C:1576], float(NB)))
            DVE.wait(m)
            m = DVE.mark(v.tensor_copy(HI[d][:, 0:C], TMPI))
            DVE.wait(m, m1)
            js = [None, None]
            for b in range(NBIN):
                DVE.wait(js[b % 2])
                m = js[b % 2] = DVE.mark(v.tensor_scalar(JUNK[b % 2][:, 0:C], HI[d][:, 0:C], float(b), 0.0, ALU.is_equal, ALU.add,
                                             accum_out=CNT[:, d, b:b + 1]))
            PE.wait(m, m_c)
            PE.mark(t.matmul(PS[5][:, 0:NBIN], TRI[:], CNT[:, d, :], start=True, stop=True))
            PE.mark(t.matmul(PS[5][:, 128:128 + NB], ONE[:], CNT[:, d, 0:NB], start=True, stop=True))
            m = PE.mark(t.matmul(PS[6][0:NB, 0:1], CNT[:, d, 0:NB], ONE[:, 0:1], start=True, stop=True))
            DVE.wait(m)
            tiles, si = SM[:, d, 0:NB], SMI[:, d, 0:NB]
            ct, ci = SC[0:NB, d, 0:1], SCI[0:NB, d, 0:1]
            DVE.mark(v.tensor_scalar(si, PS[5][:, 128:128 + NB], 127.0, None, ALU.add))
            m = DVE.mark(v.tensor_scalar(ci, PS[6][0:NB, 0:1], 127.0, None, ALU.add))
            DVE.wait(m)
            DVE.mark(v.tensor_scalar(si, si, 7, None, ALU.logical_shift_right))
            m = DVE.mark(v.tensor_scalar(ci, ci, 7, None, ALU.logical_shift_right))
            DVE.wait(m)
            DVE.mark(v.tensor_scalar(ct, ci, 1.0, None, ALU.max))
            m = DVE.mark(v.tensor_scalar(tiles, si, 1.0, None, ALU.max))
            PE.wait(m)
            mts = PE.mark(t.matmul(PS[6][0:NB, 8:9], TRI[0:NB, 0:NB], ct, start=True, stop=True))
            z = SM[:, 2 + d, 0:NB]
            mz = DVE.mark(v.memset(z, 0.0))
            DVE.wait(mz)
            cum = BASE[:, d, 0:NB]
            m = DVE.mark(v.tensor_tensor_scan(cum, tiles, z, 0.0, ALU.add, ALU.add))
            DVE.wait(m)
            m = DVE.mark(v.tensor_tensor(z, cum, tiles, ALU.subtract))
            DVE.wait(m)
            m = DVE.mark(v.scalar_tensor_tensor(cum, z, 128.0, PS[5][:, 0:NB], ALU.mult, ALU.add))
            DVE.mark(v.memset(BASE[:, d, NB:NBIN], float(NT * P)))
            DVE.wait(mts)
            m = DVE.mark(v.tensor_copy(SC[0:NB, d, 1:2], PS[6][0:NB, 8:9]))
            DVE.wait(m)
            mb = DVE.mark(v.tensor_scalar(GE[0:NB, :], IOTT[0:NB, :], SC[0:NB, d, 1:2], None, ALU.is_ge))
            PE.wait(mb)
            for i in range(4):
                n = min(512, NTP - 512 * i)
                mp = PE.mark(t.matmul(PS[i][0:1, 0:n], ONB[0:NB, 0:1], GE[0:NB, 512 * i:512 * i + n],
                                      start=True, stop=True))
            DVE.wait(mp)
            for i in range(4):
                n = min(512, NTP - 512 * i)
                m = DVE.mark(v.tensor_scalar(BT[32 * d:32 * d + 1, 512 * i:512 * i + n], PS[i][0:1, 0:n],
                                             -1.0, 128.0, ALU.add, ALU.mult))
            table = m

            R = PS[4][:, 0:W5 * NBIN].rearrange("p (c b) -> p c b", b=NBIN)
            oh_mark, free = {}, {}

            def onehot(q):
                o = OH[q % 4]
                DVE.wait(free.get(q - 4))
                for c in range(W5):
                    m = DVE.mark(v.tensor_scalar(o[:, c, :], IOTA[:, 0:NBIN],
                                                 HI[d][:, W5 * q + c:W5 * q + c + 1], None, ALU.is_equal))
                oh_mark[q] = m

            def add(to, rhs, start=False):
                return PE.mark(t.matmul(to, IDB[:], rhs, start=start, stop=True, skip_group_check=True))

            onehot(0)
            onehot(1)
            PE.wait(m, oh_mark[1])
            PE.mark(t.matmul(R, IDN[:], BASE[:, d, :].unsqueeze(1).broadcast_to([P, W5, NBIN]), start=True,
                             stop=True, skip_group_check=True))
            for c in range(W5 - 1):
                mr = add(R[:, c + 1:W5, :], OH[0][:, c, :].unsqueeze(1).broadcast_to([P, W5 - 1 - c, NBIN]))
            for q in range(NG5):
                k, j = q // CH, q % CH
                if j == 0:
                    DVE.wait(ready.get(k - 2))
                DVE.wait(mr)
                mm = DVE.mark(v.tensor_tensor(PRD[q % 2], R, OH[q % 4], ALU.mult))
                if q + 1 < NG5:
                    PE.wait(mm, oh_mark[q + 1])
                    a, b = OH[q % 4], OH[(q + 1) % 4]
                    for e in range(W5):
                        mr = add(R[:, 0:W5 - e, :], a[:, e:W5, :])
                        if e:
                            mr = add(R[:, W5 - e:W5, :], b[:, 0:e, :])
                    free[q] = mr
                if q + 2 < NG5:
                    onehot(q + 2)
                DVE.wait(mm)
                m = DVE.mark(v.tensor_reduce(RNK[k % 2][:, W5 * j:W5 * j + W5], PRD[q % 2],
                                             mybir.AxisListType.X, ALU.add))
                if j == CH - 1 or q == NG5 - 1:
                    w = W5 * (j + 1)
                    ri = RKI[k % 2]
                    DVE.wait(m)
                    m = DVE.mark(v.tensor_copy(ri[:, 0, 0:w], RNK[k % 2][:, 0:w]))
                    DVE.wait(m)
                    DVE.mark(v.tensor_scalar(ri[:, 1, 0:w], ri[:, 0, 0:w], 127, None, ALU.bitwise_and))
                    m = DVE.mark(v.tensor_scalar(ri[:, 2, 0:w], ri[:, 0, 0:w], 7, None, ALU.logical_shift_right))
                    DVE.wait(m)
                    u = min(w, C - CW * k)
                    m = DVE.mark(v.scalar_tensor_tensor(place[:, CW * k:CW * k + u], ri[:, 1, 0:u], float(NTP),
                                                        ri[:, 2, 0:u], ALU.mult, ALU.add))
                    yield k, u, m, table

        DVE.wait(got_idx)
        m = DVE.mark(v.tensor_scalar(TMPI, DSTi, 127, None, ALU.bitwise_and))
        DVE.mark(v.tensor_copy(RECB[:, :, 0].bitcast(I32), SRCi))
        DVE.wait(m)
        DVE.mark(v.tensor_copy(RECB[:, :, 1], TMPI))
        m_recb = DVE.mark(v.tensor_scalar(RECB[:, :, 2], TYPi, 0.0, 8.0, ALU.max, ALU.min))
        l_sb = lane("l_sb")
        POOL.wait(null_b, m_recb)
        for k, u, m, table_b in sort(0, DSTi, POSB, {}):
            POOL.wait(m)
            for c in range(CW * k, CW * k + u):
                done_b = l_sb.mark(g.indirect_dma_start(
                    out=RBd, out_offset=bass.IndirectOffsetOnAxis(ap=POSB[:, c:c + 1], axis=0),
                    in_=RECB[:, c, :], in_offset=None))
        DVE.roll()
        PE.roll()
        DVE.wait(got_idx)
        place_a = []
        for k, u, m, table_a in sort(1, SRCi, POSA, {}):
            place_a.append((k, u, m))
        DVE.done()
        m = DVE.mark(v.tensor_scalar(TMPI, SRCi, 127, None, ALU.bitwise_and))
        DVE.wait(m)
        m_rels = DVE.mark(v.tensor_copy(RELS[:, 0:C], TMPI))

        DVE.wait(got_w)
        m = DVE.mark(v.tensor_tensor(EB[32:41, 0, :], EB[32:41, 0, :], EB[32:41, 1, :], ALU.add))
        DVE.mark(v.tensor_tensor(BR[0:1, 2, 0:256], BR[0:1, 0, 0:256], BR[0:1, 1, 0:256], ALU.add))
        DVE.mark(v.tensor_copy(BR[0:1, 2, 256:384], BR[0:1, 0, 256:384]))
        m_eb = DVE.mark(v.tensor_copy(BR[0:1, 2, 384:512], BR[0:1, 1, 256:384]))
        PE.wait(got_w)
        for i in range(3):
            w = W1A[:, 0, :] if i == 0 else W1B[:, i - 1, :]
            m = PE.mark(t.matmul(PS[5 + i][0:17, 0:256], EC[:, 17 * i:17 * i + 17], w, start=True, stop=True))
        DVE.wait(m)
        for i in range(3):
            m_mm = DVE.mark(v.tensor_copy(MM[:, i, :], PS[5 + i][0:17, 0:256]))
        ACE.wait(got_w, m_c)
        for i in range(3):
            m = ACE.mark(s.activation(SCL[:, i, 0:2], PV[:, 11 * i + 6:11 * i + 8], ACT.Sqrt, bias=EP[:, 0:1]))
        DVE.wait(m)
        for i in range(3):
            m = DVE.mark(v.reciprocal(SCL[:, i, 0:2], SCL[:, i, 0:2]))
        DVE.wait(m)
        for i in range(3):
            m = DVE.mark(v.tensor_tensor(SCL[:, i, 0:2], SCL[:, i, 0:2], PV[:, 11 * i:11 * i + 2], ALU.mult))
            DVE.mark(v.tensor_tensor(SCL[:, i, 2:4], PV[:, 11 * i + 8:11 * i + 10], PV[:, 11 * i + 4:11 * i + 6],
                                     ALU.subtract))
        m = DVE.mark(v.tensor_scalar(V17[:, 0:1], DIF[0:17, 0:1], 0.0, None, ALU.is_equal))
        DVE.mark(v.tensor_scalar(V17[:, 1:2], DIF[0:17, 0:1], -16.0, None, ALU.is_equal))
        DVE.done()
        m = DVE.mark(v.memset(AGG, 0.0))
        DVE.wait(m)
        DVE.mark(v.tensor_tensor(V17[:, 2:3], V17[:, 0:1], V17[:, 1:2], ALU.add))
        for i in range(3):
            m = DVE.mark(v.tensor_tensor(SCL[:, i, 2:4], SCL[:, i, 2:4], SCL[:, i, 0:2], ALU.mult))
        DVE.wait(m)
        for i in range(3):
            m_scl = DVE.mark(v.tensor_tensor(SCL[:, i, 2:4], SCL[:, i, 2:4], PV[:, 11 * i + 2:11 * i + 4], ALU.add))
        DVE.wait(done_b, null_a, null_b, m_scl)
        DVE.wait(DVE.mark(v.memset(BIG[32:41, NP:2 * NP], 0.0)))
        DVE.wait(DVE.mark(v.memset(BIG[0:17, NP:2 * NP], 0.0)))
        m_tz = DVE.mark(v.tensor_scalar(T17, T17, V17[:, 2:3], None, ALU.add))
        DVE.wait(m_tz)

        slots = [lane(f"l_g{i}") for i in range(4)]

        def aggregate(tag, table, bt_row, rows, idx, rel, idx_ready, small):
            used, got, mm, added = {}, {}, {}, {}
            last_add = [None]
            DVE.wait(table)

            def adds(q):
                n = min(GT, NT - GT * q)
                ins, offs = nc.values_load_multi_w_load_instructions(
                    BT[bt_row:bt_row + 1, GT * q:GT * q + n], engines=(mybir.EngineType.DVE,), min_val=0,
                    max_val=(NB - 1) * P,
                    skip_runtime_bounds_check_because="a count of bucket starts, times 128")
                DVE.wait(mm[q])
                b = q % 2
                m = prev = last_add[0]
                for j in range(n):
                    win = AGG[:, bass.ds(offs[j], P)]
                    DVE.wait(prev)
                    prev = DVE.mark(v.tensor_tensor(win, win, PS[b][:, j * P:(j + 1) * P], ALU.add))
                    if small:
                        lo_, n_, base_ = small[0], small[1], BIG[small[0]:small[0] + small[1], NP:2 * NP]
                        win = base_[:, bass.ds(offs[j], P)]
                        DVE.wait(m)
                        m = DVE.mark(v.tensor_tensor(win, win, PS[2 + b][lo_:lo_ + n_, j * P:(j + 1) * P],
                                                     ALU.add))
                last_add[0] = prev
                if small:
                    last_add[0] = m
                added[q] = last_add[0]

            for q in range(NGR):
                n = min(GT, NT - GT * q)
                sl, b = q % 4, q % 2
                POOL.wait(mm.get(q - 4), idx_ready(q))
                for j in range(n):
                    c = GT * q + j
                    got[q] = slots[sl].mark(g.indirect_dma_start(
                        out=G[:, sl, j, :], out_offset=None, in_=rows,
                        in_offset=bass.IndirectOffsetOnAxis(ap=idx(c), axis=0)))
                DVE.wait(mm.get(q - 4), idx_ready(q))
                for j in range(n):
                    ms = DVE.mark(v.tensor_scalar(S[:, sl, j, :], IOTA[:], rel(GT * q + j), None, ALU.is_equal))
                if small and small[3]:
                    for j in range(n):
                        ms = DVE.mark(small[3](q, j))
                if q:
                    adds(q - 1)
                PE.wait(got[q], ms, added.get(q - 2))
                for j in range(n):
                    m = PE.mark(t.matmul(PS[b][:, j * P:(j + 1) * P], G[:, sl, j, :], S[:, sl, j, :],
                                         start=True, stop=True))
                    if small:
                        m = PE.mark(t.matmul(PS[2 + b][small[0]:small[0] + small[1], j * P:(j + 1) * P],
                                             small[2](q, j), S[:, sl, j, :], start=True, stop=True))
                mm[q] = m
            adds(NGR - 1)
            return added[NGR - 1], mm[NGR - 1]

        l_rb = lane("l_rb")
        SP.wait(done_b)
        got_rb = l_rb.mark(nc.sync.dma_start(RBs, RBv))
        for q_ in (DVE, PE, POOL):
            q_.roll()
        agg_done, mm_done = aggregate(
            "a", table_b, 0, x, lambda c: RBs[:, c, 0:1].bitcast(I32), lambda c: RBs[:, c, 1:2], lambda q: got_rb,
            (32, 9, lambda q, j: OT[q % 4][:, j, :],
             lambda q, j: v.tensor_scalar(OT[q % 4][:, j, :], IOTA[:, 0:9], RBs[:, GT * q + j, 2:3], None,
                                          ALU.is_equal)))

        for q_ in (DVE, PE, POOL, ACE):
            q_.roll()
        l_ea = [lane(f"l_ea{i}") for i in range(2)]
        l_sa = [lane(f"l_sa{i}") for i in range(2)]
        scat_a = {}
        for i in range(2):
            m_one = DVE.mark(v.memset(RECA[i][:, :, 18:20], 1.0))
        ea_v = ea.rearrange("p (c w) -> p c w", w=16)
        ea_free = {}

        def records(k):
            _, u, pm = place_a[k]
            i = k % 2
            c0 = CW * k
            SP.wait(ea_free.get(k - 2))
            m = l_ea[i].mark(nc.sync.dma_start(EAR[i][:, 0:u, :], ea_v[:, c0:c0 + u, :]))
            ACE.wait(m, scat_a.get(k - 2), m_rels, m_one)
            ACE.mark(s.copy(RECA[i][:, 0:u, 2:18], EAR[i][:, 0:u, :]))
            ACE.mark(s.copy(RECA[i][:, 0:u, 0].bitcast(I32), DSTi[:, c0:c0 + u]))
            m = ACE.mark(s.copy(RECA[i][:, 0:u, 1], RELS[:, c0:c0 + u]))
            ea_free[k] = m
            POOL.wait(m, pm, null_a)
            for c in range(u):
                scat_a[k] = l_sa[i].mark(g.indirect_dma_start(
                    out=RAd, out_offset=bass.IndirectOffsetOnAxis(ap=POSA[:, c0 + c:c0 + c + 1], axis=0),
                    in_=RECA[i][:, c, :], in_offset=None))

        records(0)

        l_xb = [lane(f"l_xb{i}") for i in range(4)]
        l_x1 = [lane(f"l_x1{i}") for i in range(2)]
        free_xb, free_xm, free_ps, free_g, store = {}, {}, {}, {}, {}
        GB = 14
        xv = x.rearrange("(b p) f -> b p f", p=P)
        x1v = X1d.rearrange("(b p) f -> p b f", p=P)
        SP.wait(agg_done, mm_done)
        DVE.wait(mm_done)
        ACE.wait(agg_done, mm_done)
        PE.wait(agg_done, m_eb)
        rec_next = [1]
        agg_init = None
        tr_free = {}
        for gr in range(NB // GB):
            yb = Y[gr % 2]
            st = ST[gr % 2]
            for bi in range(GB):
                b = gr * GB + bi
                sl, s2 = b % 4, b % 2
                col = slice(b * P, (b + 1) * P)
                SP.wait(free_xb.get(b - 4))
                mx = l_xb[sl].mark(nc.sync.dma_start(XB[sl], xv[b]))
                PE.wait(mx, free_ps.get(b - 2))
                t4 = PS[4 + s2]
                PE.mark(t.transpose(t4[:, 0:P], XB[sl], IDN[:]))
                PE.mark(t.matmul(t4[:, P:2 * P], WM[:], AGG[:, col], start=True, stop=False))
                m = PE.mark(t.matmul(t4[:, P:2 * P], EB[32:41, 0, :], T9[:, col], start=False, stop=True))
                ACE.wait(m, free_xm.get(b - 2))
                m = ACE.mark(s.copy(XMT[s2], t4[:, 0:2 * P]))
                free_ps[b] = m
                gb = PS[6 + s2]
                PE.wait(m, free_g.get(b - 2))
                PE.mark(t.matmul(gb[:, :], ONE[0:1, :], BR[0:1, 2, :], start=True, stop=False))
                PE.mark(t.matmul(gb[:, 0:384], XMT[s2][:, P:2 * P], WI[:], start=False, stop=False))
                PE.mark(t.matmul(gb[:, 0:256], XMT[s2][:, 0:P], WH[:, 0:256], start=False, stop=False))
                m = PE.mark(t.matmul(gb[:, 384:512], XMT[s2][:, 0:P], WH[:, 256:384], start=False, stop=True))
                free_xm[b] = m
                ACE.wait(m, free_g.get(b - 2))
                mrz = ACE.mark(s.activation(RZ[s2], gb[:, 0:256], ACT.Sigmoid))
                DVE.wait(mrz)
                d, e = DD[s2][:, 0:P], DD[s2][:, P:2 * P]
                m = DVE.mark(v.tensor_tensor(d, RZ[s2][:, 0:P], gb[:, 384:512], ALU.mult))
                DVE.wait(m)
                m = DVE.mark(v.tensor_tensor(d, d, gb[:, 256:384], ALU.add))
                ACE.wait(m)
                mt = ACE.mark(s.activation(TN[s2], d, ACT.Tanh))
                DVE.wait(mt)
                m1 = DVE.mark(v.tensor_tensor(d, XB[sl], TN[s2], ALU.subtract))
                m2 = DVE.mark(v.tensor_tensor(e, XB[sl], TN[s2], ALU.add))
                DVE.wait(m1)
                m = DVE.mark(v.tensor_tensor(d, d, RZ[s2][:, P:2 * P], ALU.mult))
                DVE.wait(m)
                free_xb[b] = m
                m = DVE.mark(v.tensor_tensor(yb[:, bi, :], d, e, ALU.add))
                free_g[b] = m
                DVE.wait(m)
                m = DVE.mark(v.bn_stats(st[:, bi, 0:6], yb[:, bi, :]))
                DVE.wait(m)
                mst = DVE.mark(v.bn_aggr(st[:, bi, 6:8], st[:, bi, 0:6]))
                if b % 3 == 2 and rec_next[0] < NCH:
                    records(rec_next[0])
                    rec_next[0] += 1
            ACE.wait(mst)
            m = ACE.mark(s.activation(st[:, :, 7], st[:, :, 7], ACT.Sqrt, bias=EP[:, 0:1]))
            DVE.wait(m)
            m = DVE.mark(v.reciprocal(st[:, :, 7], st[:, :, 7]))
            DVE.wait(m)
            for bi in range(GB):
                m = DVE.mark(v.tensor_scalar(yb[:, bi, :], yb[:, bi, :], st[:, bi, 6:7], st[:, bi, 7:8],
                                             ALU.subtract, ALU.mult))
            SP.wait(m)
            PE.wait(m)
            store[gr] = l_x1[gr % 2].mark(nc.sync.dma_start(x1v[:, gr * GB:(gr + 1) * GB, :], yb))
            for bi in range(GB):
                b = gr * GB + bi
                pt = PS[bi % 2]
                PE.wait(tr_free.get(b - 2))
                m = PE.mark(t.transpose(pt[:, 0:P], yb[:, bi, :], IDN[:]))
                ACE.wait(m)
                agg_init = ACE.mark(s.copy(AGG[:, b * P:(b + 1) * P], pt[:, 0:P]))
                tr_free[b] = agg_init
            DVE.wait(store.get(gr - 1), agg_init)
        while rec_next[0] < NCH:
            records(rec_next[0])
            rec_next[0] += 1

        l_ra = [lane(f"l_ra{i}") for i in range(3)]
        l_ho = [lane(f"l_ho{i}") for i in range(2)]
        l_xo = [lane(f"l_xo{i}") for i in range(2)]
        l_out = [lane(f"l_out{i}") for i in range(2)]
        tables = [X1d, H1d, H2d]
        all_scat = [scat_a[NCH - 1], scat_a[NCH - 2]]
        wrote = [store[NB // GB - 1], store[NB // GB - 2]]
        ra_mark, ix_mark, ra_last = {}, {}, {}
        for lay in range(3):
            for q_ in (DVE, PE, POOL, ACE):
                q_.roll()
            POOL.wait(*wrote)
            DVE.wait(agg_init, *wrote)
            if lay == 0:
                SP.wait(*all_scat)
                NRC = NTP // RC
                pe_used = {}

                def chunk(i):
                    SP.wait(pe_used.get(i - 3), ix_mark.get(i - 3))
                    m = l_ra[i % 3].mark(nc.sync.dma_start(RAR[i % 3], RAv[:, RC * i:RC * (i + 1), :]))
                    ra_mark[i] = m
                    ACE.wait(m)
                    ACE.mark(s.copy(IDXA[:, RC * i:RC * (i + 1)], RAR[i % 3][:, :, 0].bitcast(I32)))
                    ix_mark[i] = ACE.mark(s.copy(RELA[:, RC * i:RC * (i + 1)], RAR[i % 3][:, :, 1]))

                chunk(0)
                chunk(1)

                def ready_a(q):
                    i = q * GT // RC
                    if (q * GT) % RC == 0 and q:
                        pe_used[i - 1] = (PE.sem, PE.n, f"{PE.name}{PE.k}")
                    if (q * GT) % RC == 0 and i + 1 < NRC and i + 1 not in ix_mark:
                        chunk(i + 1)
                    return ix_mark[i]

                small = (0, 17, lambda q, j: RAR[(q * GT // RC) % 3][:, (q * GT + j) % RC, 2:19], None)
            else:
                def ready_a(q):
                    return None
                small = None
            agg_done, mm_done = aggregate(
                "b", table_a, 32, tables[lay], lambda c: IDXA[:, c:c + 1], lambda c: RELA[:, c:c + 1], ready_a,
                small)
            PE.wait(agg_done, m_mm)
            ACE.wait(agg_done, mm_done)
            DVE.wait(mm_done)
            fin = lay == 2
            hid_f, out_f, tr_f, sto, ot_f, trs_f, xo_m, y_f = {}, {}, {}, {}, {}, {}, {}, {}
            nk = (NP + 511) // 512
            hv = None if fin else tables[lay + 1].rearrange("(b p) f -> p b f", p=P)
            for k in range(nk):
                w = min(512, NP - 512 * k)
                nb = w // P
                col = slice(512 * k, 512 * k + w)
                s2 = k % 2
                if fin:
                    SP.wait(y_f.get(k - 2))
                    xo_m[k] = l_xo[s2].mark(nc.sync.dma_start(XO[s2][:, 0:nb, :], x1v[:, 4 * k:4 * k + nb, :]))
                for h in range(2):
                    bank = PS[4 + h]
                    PE.wait(hid_f.get((k - 1, h)))
                    PE.mark(t.matmul(bank[:, 0:w], W1A[:, lay, h * P:(h + 1) * P], AGG[:, col], start=True,
                                     stop=False))
                    m = PE.mark(t.matmul(bank[:, 0:w], MM[:, lay, h * P:(h + 1) * P], T17[:, col], start=False,
                                         stop=True))
                    ACE.wait(m, out_f.get(k - 2), m_scl)
                    hid_f[(k, h)] = mh = ACE.mark(s.activation(HID[s2][:, h, 0:w], bank[:, 0:w], ACT.Relu,
                                                               bias=SCL[:, lay, 2 + h:3 + h],
                                                               scale=SCL[:, lay, h:h + 1]))
                PE.wait(mh, ot_f.get(k - 1))
                PE.mark(t.matmul(PS[6][:, 0:w], W2[:, lay, 0, :], HID[s2][:, 0, 0:w], start=True, stop=False))
                m = PE.mark(t.matmul(PS[6][:, 0:w], W2[:, lay, 1, :], HID[s2][:, 1, 0:w], start=False, stop=True))
                out_f[k] = m
                ACE.wait(m)
                b2 = PV[:, 11 * lay + 10:11 * lay + 11]
                m = ACE.mark(s.activation(AGG[:, col], PS[6][:, 0:w], ACT.Identity if fin else ACT.Relu, bias=b2))
                ot_f[k] = agg_init = m
                PE.wait(m, trs_f.get(k - 1))
                for j in range(nb):
                    m = PE.mark(t.transpose(PS[7][:, j * P:(j + 1) * P],
                                            AGG[:, 512 * k + j * P:512 * k + (j + 1) * P], IDN[:]))
                DVE.wait(m, sto.get(k - 2))
                if not fin:
                    m = DVE.mark(v.tensor_copy(TRS[s2][:, 0:nb, :].rearrange("p a b -> p (a b)"), PS[7][:, 0:w]))
                    trs_f[k] = m
                    SP.wait(m)
                    sto[k] = l_ho[s2].mark(nc.sync.dma_start(hv[:, 4 * k:4 * k + nb, :], TRS[s2][:, 0:nb, :]))
                    continue
                y = TRS[s2]
                st = ST2[s2]
                DVE.wait(xo_m[k])
                m = DVE.mark(v.tensor_tensor(y[:, 0:nb, :].rearrange("p a b -> p (a b)"),
                                             XO[s2][:, 0:nb, :].rearrange("p a b -> p (a b)"), PS[7][:, 0:w],
                                             ALU.add))
                trs_f[k] = y_f[k] = m
                DVE.wait(m)
                for j in range(nb):
                    m = DVE.mark(v.bn_stats(st[:, j, 0:6], y[:, j, :]))
                DVE.wait(m)
                for j in range(nb):
                    m = DVE.mark(v.bn_aggr(st[:, j, 6:8], st[:, j, 0:6]))
                ACE.wait(m)
                m = ACE.mark(s.activation(st[:, 0:nb, 7], st[:, 0:nb, 7], ACT.Sqrt, bias=EP[:, 0:1]))
                DVE.wait(m)
                m = DVE.mark(v.reciprocal(st[:, 0:nb, 7], st[:, 0:nb, 7]))
                DVE.wait(m)
                for j in range(nb):
                    m = DVE.mark(v.tensor_scalar(y[:, j, :], y[:, j, :], st[:, j, 6:7], st[:, j, 7:8],
                                                 ALU.subtract, ALU.mult))
                SP.wait(m)
                full = min(nb, (N - 512 * k) // P)
                if full:
                    sto[k] = l_out[s2].mark(nc.sync.dma_start(
                        out[512 * k:512 * k + full * P, :].rearrange("(b p) f -> p b f", p=P), y[:, 0:full, :]))
                rest = min(w, N - 512 * k) - full * P
                if rest:
                    sto[k] = l_out[s2].mark(nc.sync.dma_start(
                        out[512 * k + full * P:512 * k + full * P + rest, :], y[0:rest, full, :]))
            wrote = [sto[nk - 1], sto[nk - 2]]
        SP.wait(*wrote)


_SHAPE = (12500, 128)


def _layout(i):
    import numpy as np
    rows = NP - N

    def edges(a, fill):
        a = np.concatenate([a, np.full((P * C - E,) + a.shape[1:], fill, a.dtype)])
        return np.ascontiguousarray(a.reshape(P, -1))

    def cols(a):
        return a.reshape(2, P).T

    pv = []
    for k in range(3):
        for n in ("g", "be", "rm", "rv", "b1"):
            pv.append(cols(i[f"L1_gnn_{n}0"] if k == 0 and n != "b1" else i["L1_gnn_b1_0"] if k == 0
                           else i[f"L1_gnn_{n}"][k - 1]))
        pv.append((i["L1_gnn_b2_0"] if k == 0 else i["L1_gnn_b2"][k - 1]).reshape(P, 1))
    enc = [np.concatenate([i["L1_gnn_enc_w0"], i["L1_gnn_enc_b0"][None]])]
    for k in range(2):
        enc.append(np.concatenate([i["L1_gnn_enc_w"][k], i["L1_gnn_enc_b"][k][None]]))
    w1 = i["L1_gnn_w1"]
    w2 = [i["L1_gnn_w2_0"], i["L1_gnn_w2"][0], i["L1_gnn_w2"][1]]
    d = {
        "x": np.concatenate([i["x"], np.zeros((rows, P), i["x"].dtype)]),
        "dst": edges(i["dst"], NP), "src": edges(i["src"], NP), "typ": edges(i["edge_type_9"], 0),
        "ea": edges(i["edge_attr_16"], 0),
        "wmsgT": i["L0_gnn_W_msg"].T, "wihT": i["L0_gnn_W_ih"].T, "whhT": i["L0_gnn_W_hh"].T,
        "emb": i["L0_gnn_edge_embed"], "bmsg": i["L0_gnn_b_msg"][None], "bih": i["L0_gnn_b_ih"][None],
        "bhh": i["L0_gnn_b_hh"][None],
        "encT": np.concatenate([e.T for e in enc], axis=1),
        "w1a": np.concatenate([i["L1_gnn_w1_0"], w1[0, 0:P], w1[1, 0:P]], axis=1),
        "w1b": np.concatenate([w1[0, P:], w1[1, P:]], axis=1),
        "w2": np.concatenate([w[k * P:(k + 1) * P] for w in w2 for k in range(2)], axis=1),
        "pv": np.concatenate(pv, axis=1),
    }
    return {k: np.ascontiguousarray(a) for k, a in d.items()}


def kernel(**inputs):
    import numpy as np
    import concourse.bacc as bacc
    from concourse.bass_utils import run_bass_kernel_spmd

    nc = bacc.Bacc("TRN2", target_bir_lowering=False, num_devices=1)
    arrays, args = {}, []
    for name, a in _layout({k: np.asarray(a) for k, a in inputs.items()}).items():
        arrays[f"in_{name}"] = a
        args.append(nc.dram_tensor(f"in_{name}", a.shape, mybir.dt.from_np(a.dtype), kind="ExternalInput").ap())
    args.append(nc.dram_tensor("out_0", _SHAPE, F32, kind="ExternalOutput").ap())
    program(nc, *args)
    r = run_bass_kernel_spmd(nc, [arrays], core_ids=[0])
    return r.results[0]["out_0"]
```

```python
import concourse.bass as bass
from concourse import mybir
from concourse.alu_op_type import AluOpType as ALU
from contextlib import ExitStack

F32 = mybir.dt.float32
BF16 = mybir.dt.bfloat16
I32 = mybir.dt.int32
ACT = mybir.ActivationFunctionType

P = 128
N = 12500
NB = 98
NP = NB * P
NX = NP + P
E = 200000
C = 1563
NT = C + NB
NTP = 1664
NTF = 1624
W0 = 64
NBIN = NB + 1
W5 = 5
NG5 = 313
CH = 8
CW = CH * W5
NCH = (NG5 + CH - 1) // CH
RW = 20
EPS = 1e-5
GT = 4
GB = 7
RC = 64
PACE = 16.45
SLACK = 16


def when(k):
    last = min(4 * k + 4, NB)
    return NTF if last == NB else min(NTF, int(PACE * last) + SLACK)


class Queue:

    def __init__(self, ctx, nc, eng, name):
        self.ctx, self.nc, self.eng, self.name = ctx, nc, eng, name
        self.k, self.n, self.seen, self.held = 0, 0, {}, None
        self.sem = ctx.enter_context(nc.semaphore(f"{name}0"))

    def roll(self):
        self.k += 1
        self.n = 0
        self.sem = self.ctx.enter_context(self.nc.semaphore(f"{self.name}{self.k}"))

    def do(self, sem, by, call, *a, **k):
        if self.held is None:
            ins = call(*a, **k)
            if sem is not None:
                ins.then_inc(sem, by)
        else:
            self.held.append((sem, by, call, a, k))

    def write_out(self, held):
        for sem, by, call, a, k in held:
            self.do(sem, by, call, *a, **k)

    def last(self):
        return (self.sem, self.n, f"{self.name}{self.k}") if self.n else None

    def mark(self, call, *a, **k):
        self.do(self.sem, 1, call, *a, **k)
        self.n += 1
        return self.last()

    def done(self):
        self.wait(self.last())

    def wait(self, *marks):
        for m in marks:
            if m is not None and self.seen.get(m[2], 0) < m[1]:
                self.do(None, 0, self.eng.wait_ge, m[0], m[1])
                self.seen[m[2]] = m[1]


class Lane:

    def __init__(self, ctx, nc, name):
        self.sem, self.n, self.name = ctx.enter_context(nc.semaphore(name)), 0, name

    def mark(self, queue, call, *a, **k):
        queue.do(self.sem, 16, call, *a, **k)
        self.n += 16
        return (self.sem, self.n, self.name)


def program(nc, x, dst, src, typ, ea, wmsgT, wihT, whhT, emb, bmsg, bih, bhh, encT, w1a, w1b, w2, pv, out):
    ctx = ExitStack()
    with ctx:
        def sb(name, shape, dt=F32):
            return ctx.enter_context(nc.sbuf_tensor(name, shape, dt))

        lanes = []

        def lane(name):
            lanes.append(Lane(ctx, nc, name))
            return lanes[-1]

        DVE = Queue(ctx, nc, nc.vector, "dve")
        ACE = Queue(ctx, nc, nc.scalar, "act")
        PE = Queue(ctx, nc, nc.tensor, "pe")
        POOL = Queue(ctx, nc, nc.gpsimd, "pool")
        SP = Queue(ctx, nc, nc.sync, "sp")
        engines = ((DVE, mybir.EngineType.DVE), (ACE, mybir.EngineType.Activation), (PE, mybir.EngineType.PE),
                   (POOL, mybir.EngineType.Pool), (SP, mybir.EngineType.SP))
        v, s, t, g = nc.vector, nc.scalar, nc.tensor, nc.gpsimd

        RBd = nc.dram_tensor("rec_b", (P * NTP, 3), F32).ap()
        RAd = nc.dram_tensor("rec_a", (P * NTP, RW), F32).ap()
        X1d = nc.dram_tensor("x1_rows", (NP, P), F32).ap()
        H1d = nc.dram_tensor("h1_rows", (NP, P), F32).ap()
        H2d = nc.dram_tensor("h2_rows", (NP, P), F32).ap()

        BIG = sb("BIG", [P, 2 * NX])
        XR = sb("XR", [P, 6800])
        DR = sb("DR", [P, 8192])
        SRCi = sb("SRCi", [P, C], I32)[:, :]
        FL = sb("FL", [1, 8], I32)
        FW = sb("FW", [P, 8])
        BT = BIG[64:97, NX + 9600:NX + 9600 + NTP].bitcast(I32)
        G = sb("G", [P, 4, GT, P])
        S = sb("S", [P, 4, GT, P])
        WM = sb("WM", [P, P])
        WI = sb("WI", [P, 384])
        WH = sb("WH", [P, 384])
        EC = sb("EC", [P, 51])
        W1A = sb("W1A", [P, 3, 256])
        W1B = sb("W1B", [P, 2, 256])
        W2 = sb("W2", [P, 3, 2, P])
        MM = sb("MM", [17, 3, 256])
        EB = sb("EB", [64, 2, P])
        PV = sb("PV", [P, 33])
        SCL = sb("SCL", [P, 3, 4])
        BR = BIG[64:65, NX + 8000:NX + 9536].rearrange("p (a n) -> p a n", a=3)
        IOTA = sb("IOTA", [P, P])
        DIF = sb("DIF", [P, P])
        TRI = sb("TRI", [P, P])
        IDN = sb("IDN", [P, P])
        IDB = sb("IDB", [P, P], BF16)
        ONE = sb("ONE", [P, P])
        ONB = sb("ONB", [P, 1], BF16)
        V17 = sb("V17", [17, 4])
        CNT = sb("CNT", [P, 2, NBIN])
        BASE = sb("BASE", [P, 2, NBIN])
        SM = sb("SM", [P, 4, 100])
        SMI = sb("SMI", [P, 2, 100], I32)
        SC = sb("SC", [P, 4, 4])
        SCI = sb("SCI", [P, 2, 4], I32)
        EP = sb("EP", [P, 1])
        TEND = sb("TEND", [1, 2, NB])
        LIM = sb("LIM", [1, NB])
        ZER = sb("ZER", [P, 1])
        tables_ready = []

        AGG = BIG[:, 0:NX]
        T9 = BIG[32:41, NX:NX + NP]
        T17 = BIG[0:17, NX:NX + NP]

        def carve(base):
            at = [0]

            def take(words):
                a = at[0]
                at[0] += words
                return base[:, a:a + words]
            return take

        dq = carve(DR)
        REL0 = dq(1564)
        TYPF = dq(1564)
        dq(144)
        HI = dq(788).bitcast(BF16)
        TMPI = DR[:, 4060:4060 + C].bitcast(I32)
        JUNK = [DR[:, 4060 + 788 * i:4060 + 788 * (i + 1)].bitcast(BF16) for i in range(2)]
        GE = DR[:, 4060:4060 + NTP // 2].bitcast(BF16)
        IOTT = DR[:, 6368:6368 + NTP]
        dw = carve(DR[:, 4060:])
        OH = [dw(248).bitcast(BF16)[:, 0:W5 * NBIN].rearrange("p (c b) -> p c b", b=NBIN) for _ in range(4)]
        PRD = [dw(W5 * NBIN).rearrange("p (c b) -> p c b", b=NBIN) for _ in range(2)]
        RNK = [dw(CW) for _ in range(2)]
        RKI = [dw(3 * CW).bitcast(I32).rearrange("p (a c) -> p a c", a=3) for _ in range(2)]
        hi_ = carve(BIG[:, NX:2 * NX])
        RECB = hi_(3 * C).rearrange("p (c w) -> p c w", w=3)
        POSB = hi_(C).bitcast(I32)
        xr = carve(XR)
        POSA = xr(C).bitcast(I32)
        DSTi = xr(C).bitcast(I32)
        RELS = xr(782).bitcast(BF16)
        EAR = [xr(CW * 16).rearrange("p (c w) -> p c w", w=16) for _ in range(2)]
        RECA = [xr(CW * RW).rearrange("p (c w) -> p c w", w=RW) for _ in range(2)]
        NULA = XR[:, 3908:3908 + 52 * RW].rearrange("p (c w) -> p c w", w=RW)
        NULB = XR[:, 5188:5188 + 416 * 3].rearrange("p (c w) -> p c w", w=3)
        TYPi = G[:, :, :, :].rearrange("p a b c -> p (a b c)")[:, 0:C].bitcast(I32)
        N0B = S[:, :, :, :].rearrange("p a b c -> p (a b c)")[:, 0:C].bitcast(I32)
        xr2 = carve(XR)
        RAR = [xr2(RC * RW).rearrange("p (c w) -> p c w", w=RW) for _ in range(3)]
        IDXA = xr2(NTP).bitcast(I32)
        RELA = xr2(NTP // 2).bitcast(BF16)
        dr0 = carve(DR)
        RBs = dr0(NTP * 3).rearrange("p (c w) -> p c w", w=3)
        dr0 = carve(DR[:, 8040:])
        OT = [dr0(GT * 9).rearrange("p (c w) -> p c w", w=9) for _ in range(4)]
        dr = carve(DR)
        XB = [dr(P) for _ in range(4)]
        XMT = [dr(2 * P) for _ in range(2)]
        RZ = [dr(2 * P) for _ in range(2)]
        TN = [dr(P) for _ in range(2)]
        DD = [dr(2 * P) for _ in range(2)]
        ST = [dr(GB * 8).rearrange("p (c w) -> p c w", w=8) for _ in range(2)]
        dy = carve(DR[:, 6368:])
        Y = [dy(GB * P).rearrange("p (c w) -> p c w", w=P) for _ in range(2)]
        dr2 = carve(DR)
        HID = [dr2(1024).rearrange("p (c w) -> p c w", w=512) for _ in range(2)]
        TRS = [dr2(512).rearrange("p (c w) -> p c w", w=P) for _ in range(2)]
        XO = [dr2(512).rearrange("p (c w) -> p c w", w=P) for _ in range(2)]
        ST2 = [dr2(32).rearrange("p (c w) -> p c w", w=8) for _ in range(2)]

        PS = [ctx.enter_context(nc.psum_tensor(f"ps{i}", [P, 512], F32)) for i in range(8)]

        l_idx = lane("l_idx")
        for to, frm in ((DSTi, dst), (SRCi, src), (TYPi, typ)):
            got_idx = l_idx.mark(SP, nc.sync.dma_start, to, frm)
        l_w = lane("l_w")
        POOL.mark(g.iota, IOTA[:], [[1, P]], base=0, channel_multiplier=0, allow_small_or_imprecise_dtypes=True)
        POOL.mark(g.iota, DIF[:], [[1, P]], base=0, channel_multiplier=-1, allow_small_or_imprecise_dtypes=True)
        m_iota = POOL.mark(g.iota, IOTT, [[1, NTP]], base=0, channel_multiplier=0,
                                  allow_small_or_imprecise_dtypes=True)
        POOL.wait(got_idx)
        m_n0 = POOL.mark(g.partition_broadcast, N0B, DSTi[0:1, :])
        for to, frm in ((WM[:], wmsgT), (WI[:], wihT), (WH[:], whhT), (EC[:], encT),
                        (W1A[:], w1a.rearrange("p (i n) -> p i n", i=3)),
                        (W1B[:], w1b.rearrange("p (i n) -> p i n", i=2)),
                        (W2[:], w2.rearrange("p (i k n) -> p i k n", i=3, k=2)), (PV[:], pv),
                        (EB[32:41, 0, :], emb), (EB[32:41, 1, :], bmsg.broadcast_to([9, P])),
                        (BR[0:1, 0, 0:384], bih), (BR[0:1, 1, 0:384], bhh)):
            got_w = l_w.mark(SP, nc.sync.dma_start, to, frm)

        DVE.mark(v.memset, ONE[:], 1.0)
        DVE.mark(v.memset, EP[:], EPS)
        DVE.mark(v.memset, ONB[:], 1.0)
        m_zero = DVE.mark(v.memset, ZER[:], 0.0)
        for k in range(25):
            DVE.mark(v.memset, LIM[0:1, 4 * k:min(4 * k + 4, NB)], float(when(k)))
        m0 = DVE.mark(v.memset, NULB[:, :, :], 0.0)
        DVE.wait(m0)
        m_nb = DVE.mark(v.memset, NULB[:, :, 1:2], -1.0)
        m0 = DVE.mark(v.memset, NULA[:, :, :], 0.0)
        DVE.wait(m0)
        m_na = DVE.mark(v.memset, NULA[:, :, 1:2], -1.0)
        DVE.wait(m_iota)
        DVE.mark(v.tensor_scalar, TRI[:], DIF[:], 0.0, None, ALU.is_gt)
        DVE.mark(v.tensor_scalar, IDN[:], DIF[:], 0.0, None, ALU.is_equal)
        m_c = DVE.mark(v.tensor_scalar, IDB[:], DIF[:], 0.0, None, ALU.is_equal)
        RBv = RBd.rearrange("(p c) w -> p c w", p=P)
        RAv = RAd.rearrange("(p c) w -> p c w", p=P)

        def empty_rows(ln, i):
            return ln.mark(SP, nc.sync.dma_start, RAv[:, 52 * i:52 * (i + 1), :], NULA)

        def sort(d, SEG, place):
            DVE.wait(got_idx)
            DVE.done()
            m = DVE.mark(v.tensor_scalar, TMPI, SEG, 7, None, ALU.logical_shift_right)
            m1 = DVE.mark(v.memset, HI[:, C:1576], float(NB))
            DVE.wait(m)
            m = DVE.mark(v.tensor_copy, HI[:, 0:C], TMPI)
            DVE.wait(m, m1)
            js = [None, None]
            for b in range(NBIN):
                DVE.wait(js[b % 2])
                m = js[b % 2] = DVE.mark(v.tensor_scalar, JUNK[b % 2][:, 0:C], HI[:, 0:C], float(b), 0.0, ALU.is_equal, ALU.add,
                                             accum_out=CNT[:, d, b:b + 1])
                yield None
            PE.wait(m, m_c)
            PE.mark(t.matmul, PS[5][:, 0:NBIN], TRI[:], CNT[:, d, :], start=True, stop=True)
            PE.mark(t.matmul, PS[5][:, 128:128 + NB], ONE[:], CNT[:, d, 0:NB], start=True, stop=True)
            m = PE.mark(t.matmul, PS[6][0:NB, 0:1], CNT[:, d, 0:NB], ONE[:, 0:1], start=True, stop=True)
            DVE.wait(m)
            tiles, si = SM[:, d, 0:NB], SMI[:, d, 0:NB]
            ct, ci = SC[0:NB, d, 0:1], SCI[0:NB, d, 0:1]
            DVE.mark(v.tensor_scalar, si, PS[5][:, 128:128 + NB], 127.0, None, ALU.add)
            m = DVE.mark(v.tensor_scalar, ci, PS[6][0:NB, 0:1], 127.0, None, ALU.add)
            DVE.wait(m)
            DVE.mark(v.tensor_scalar, si, si, 7, None, ALU.logical_shift_right)
            m = DVE.mark(v.tensor_scalar, ci, ci, 7, None, ALU.logical_shift_right)
            DVE.wait(m)
            DVE.mark(v.tensor_scalar, ct, ci, 1.0, None, ALU.max)
            m = DVE.mark(v.tensor_scalar, tiles, si, 1.0, None, ALU.max)
            PE.wait(m)
            mts = PE.mark(t.matmul, PS[6][0:NB, 8:9], TRI[0:NB, 0:NB], ct, start=True, stop=True)
            z = SM[:, 2 + d, 0:NB]
            mz = DVE.mark(v.memset, z, 0.0)
            DVE.wait(mz)
            cum = BASE[:, d, 0:NB]
            m = DVE.mark(v.tensor_tensor_scan, cum, tiles, z, 0.0, ALU.add, ALU.add)
            DVE.wait(m)
            cum_end = DVE.mark(v.tensor_copy, TEND[0:1, d, :], cum[0:1, :])
            m = DVE.mark(v.tensor_tensor, z, cum, tiles, ALU.subtract)
            DVE.wait(m)
            m = DVE.mark(v.scalar_tensor_tensor, cum, z, 128.0, PS[5][:, 0:NB], ALU.mult, ALU.add)
            DVE.mark(v.memset, BASE[:, d, NB:NBIN], float(NT * P))
            DVE.wait(mts, cum_end)
            m = DVE.mark(v.tensor_copy, SC[0:NB, d, 1:2], PS[6][0:NB, 8:9])
            DVE.wait(m)
            mb = DVE.mark(v.tensor_scalar, GE[0:NB, :], IOTT[0:NB, :], SC[0:NB, d, 1:2], None, ALU.is_ge)
            for i in range(4):
                n = min(512, NTP - 512 * i)
                PE.wait(mb)
                mp = PE.mark(t.matmul, PS[7][0:1, 0:n], ONB[0:NB, 0:1], GE[0:NB, 512 * i:512 * i + n],
                             start=True, stop=True)
                DVE.wait(mp)
                mb = m = DVE.mark(v.tensor_scalar, BT[32 * d:32 * d + 1, 512 * i:512 * i + n], PS[7][0:1, 0:n],
                                  -1.0, 128.0, ALU.add, ALU.mult)
            table = m
            DVE.done()
            tables_ready.append((d, m, cum_end))
            yield None

            R = PS[4][:, 0:W5 * NBIN].rearrange("p (c b) -> p c b", b=NBIN)
            oh_mark, free = {}, {}

            def onehot(q):
                o = OH[q % 4]
                DVE.wait(free.get(q - 4))
                for c in range(W5):
                    m = DVE.mark(v.tensor_scalar, o[:, c, :], IOTA[:, 0:NBIN],
                                                 HI[:, W5 * q + c:W5 * q + c + 1], None, ALU.is_equal)
                oh_mark[q] = m

            def add(to, rhs, start=False):
                return PE.mark(t.matmul, to, IDB[:], rhs, start=start, stop=True, skip_group_check=True)

            onehot(0)
            onehot(1)
            PE.wait(m, oh_mark[1])
            PE.mark(t.matmul, R, IDN[:], BASE[:, d, :].unsqueeze(1).broadcast_to([P, W5, NBIN]), start=True,
                             stop=True, skip_group_check=True)
            for c in range(W5 - 1):
                mr = add(R[:, c + 1:W5, :], OH[0][:, c, :].unsqueeze(1).broadcast_to([P, W5 - 1 - c, NBIN]))
            for q in range(NG5):
                k, j = q // CH, q % CH
                yield None
                DVE.wait(mr)
                mm = DVE.mark(v.tensor_tensor, PRD[q % 2], R, OH[q % 4], ALU.mult)
                if q + 1 < NG5:
                    PE.wait(mm, oh_mark[q + 1])
                    a, b = OH[q % 4], OH[(q + 1) % 4]
                    for e in range(W5):
                        mr = add(R[:, 0:W5 - e, :], a[:, e:W5, :])
                        if e:
                            mr = add(R[:, W5 - e:W5, :], b[:, 0:e, :])
                    free[q] = mr
                if q + 2 < NG5:
                    onehot(q + 2)
                DVE.wait(mm)
                m = DVE.mark(v.tensor_reduce, RNK[k % 2][:, W5 * j:W5 * j + W5], PRD[q % 2],
                                             mybir.AxisListType.X, ALU.add)
                if j == CH - 1 or q == NG5 - 1:
                    w = W5 * (j + 1)
                    ri = RKI[k % 2]
                    DVE.wait(m)
                    m = DVE.mark(v.tensor_copy, ri[:, 0, 0:w], RNK[k % 2][:, 0:w])
                    DVE.wait(m)
                    DVE.mark(v.tensor_scalar, ri[:, 1, 0:w], ri[:, 0, 0:w], 127, None, ALU.bitwise_and)
                    m = DVE.mark(v.tensor_scalar, ri[:, 2, 0:w], ri[:, 0, 0:w], 7, None, ALU.logical_shift_right)
                    DVE.wait(m)
                    u = min(w, C - CW * k)
                    m = DVE.mark(v.scalar_tensor_tensor, place[:, CW * k:CW * k + u], ri[:, 1, 0:u], float(NTP),
                                                        ri[:, 2, 0:u], ALU.mult, ALU.add)
                    yield k, u, m, table

        DVE.wait(got_idx)
        m_typ = DVE.mark(v.tensor_scalar, TYPF[:, 0:C], TYPi, 0.0, 8.0, ALU.max, ALU.min)
        DVE.mark(v.tensor_copy, BT[0:1, 0:C], DSTi[0:1, :])
        m = DVE.mark(v.tensor_scalar, TMPI, SRCi, 127, None, ALU.bitwise_and)
        DVE.wait(m, m_n0)
        m = DVE.mark(v.tensor_tensor, REL0[:, 0:C], DSTi, N0B, ALU.subtract)
        m_rels = DVE.mark(v.tensor_copy, RELS[:, 0:C], TMPI)
        DVE.wait(m)
        DVE.mark(v.tensor_reduce, FW[:, 0:1], REL0[:, 0:C], mybir.AxisListType.X, ALU.max)
        m = DVE.mark(v.tensor_reduce, FW[:, 1:2], REL0[:, 0:C], mybir.AxisListType.X, ALU.min)
        DVE.wait(m)
        DVE.mark(v.tensor_scalar, FW[:, 2:3], FW[:, 0:1], float(W0), None, ALU.is_lt)
        m = DVE.mark(v.tensor_scalar, FW[:, 3:4], FW[:, 1:2], 0.0, None, ALU.is_ge)
        DVE.wait(m)
        m = DVE.mark(v.tensor_tensor, FW[:, 4:5], FW[:, 2:3], FW[:, 3:4], ALU.mult)
        PE.wait(m)
        m = PE.mark(t.matmul, PS[7][0:1, 0:1], FW[:, 4:5], ONE[:, 0:1], start=True, stop=True)
        DVE.wait(m)
        m_f1 = DVE.mark(v.tensor_scalar, FL[0:1, 0:1], PS[7][0:1, 0:1], P - 0.5, None, ALU.is_ge)
        m = DVE.mark(v.tensor_scalar, V17[:, 0:1], DIF[0:17, 0:1], 0.0, None, ALU.is_equal)
        m = DVE.mark(v.tensor_scalar, V17[:, 1:2], DIF[0:17, 0:1], -16.0, None, ALU.is_equal)
        DVE.wait(m)
        m_v17 = DVE.mark(v.tensor_tensor, V17[:, 2:3], V17[:, 0:1], V17[:, 1:2], ALU.add)

        join = ctx.enter_context(nc.semaphore("join"))
        joined = [0]

        def branch(at, ready, quick, general):
            joined[0] += len(engines)
            before = {}
            for q, kind in engines:
                q.wait(ready)
                _, vals = nc.values_load_multi_w_load_instructions(
                    FL[0:1, at:at + 1], engines=(kind,), min_val=0, max_val=1,
                    skip_runtime_bounds_check_because="the result of a comparison")
                before[q.name] = (vals[0], dict(q.seen))
            arms = []
            for form in (quick, general):
                for q, _ in engines:
                    q.seen = dict(before[q.name][1])
                    q.roll()
                    q.held = []
                del lanes[:]
                form()
                SP.wait(*((ln.sem, ln.n, ln.name) for ln in lanes))
                for q, _ in engines:
                    q.done()
                    q.do(None, 0, q.eng.sem_inc, join, 1)
                arms.append({q.name: q.held for q, _ in engines})
            for q, _ in engines:
                q.held = None
                with q.eng.If(before[q.name][0] != 0):
                    q.write_out(arms[0][q.name])
                with q.eng.Else():
                    q.write_out(arms[1][q.name])
                q.seen = dict(before[q.name][1])
                q.roll()
                q.do(None, 0, q.eng.wait_ge, join, joined[0])

        def weights():
            DVE.wait(got_w)
            m = DVE.mark(v.tensor_tensor, EB[32:41, 0, :], EB[32:41, 0, :], EB[32:41, 1, :], ALU.add)
            DVE.mark(v.tensor_tensor, BR[0:1, 2, 0:256], BR[0:1, 0, 0:256], BR[0:1, 1, 0:256], ALU.add)
            DVE.mark(v.tensor_copy, BR[0:1, 2, 256:384], BR[0:1, 0, 256:384])
            m_eb = DVE.mark(v.tensor_copy, BR[0:1, 2, 384:512], BR[0:1, 1, 256:384])
            DVE.done()
            PE.wait(got_w, m_eb)
            for i in range(3):
                w = W1A[:, 0, :] if i == 0 else W1B[:, i - 1, :]
                m = PE.mark(t.matmul, PS[5 + i][0:17, 0:256], EC[:, 17 * i:17 * i + 17], w, start=True, stop=True)
            DVE.wait(m)
            for i in range(3):
                DVE.mark(v.tensor_copy, MM[:, i, :], PS[5 + i][0:17, 0:256])
            ACE.wait(got_w, m_c)
            for i in range(3):
                m = ACE.mark(s.activation, SCL[:, i, 0:2], PV[:, 11 * i + 6:11 * i + 8], ACT.Sqrt, bias=EP[:, 0:1])
            DVE.wait(m)
            for i in range(3):
                m = DVE.mark(v.reciprocal, SCL[:, i, 0:2], SCL[:, i, 0:2])
            DVE.wait(m)
            for i in range(3):
                m = DVE.mark(v.tensor_tensor, SCL[:, i, 0:2], SCL[:, i, 0:2], PV[:, 11 * i:11 * i + 2], ALU.mult)
                DVE.mark(v.tensor_tensor, SCL[:, i, 2:4], PV[:, 11 * i + 8:11 * i + 10], PV[:, 11 * i + 4:11 * i + 6],
                                         ALU.subtract)
            DVE.done()
            for i in range(3):
                m = DVE.mark(v.tensor_tensor, SCL[:, i, 2:4], SCL[:, i, 2:4], SCL[:, i, 0:2], ALU.mult)
            DVE.wait(m)
            for i in range(3):
                m_scl = DVE.mark(v.tensor_tensor, SCL[:, i, 2:4], SCL[:, i, 2:4], PV[:, 11 * i + 2:11 * i + 4],
                                                 ALU.add)
            DVE.wait(m_scl)
            return m_eb

        def clear_types():
            return ACE.mark(s.copy, BIG[32:41, NX:2 * NX], ZER[32:41, 0:1].broadcast_to([9, NX]))

        def self_loops():
            ACE.wait(m_v17)
            ACE.mark(s.copy, T17, V17[:, 2:3].broadcast_to([17, NP]))

        ACE.wait(m_zero)
        ACE.mark(s.copy, AGG, ZER[:, 0:1].broadcast_to([P, NX]))
        m_clear = clear_types()

        def aggregate(tag, table, row, top, width, tiles, rows, idx, rel, idx_ready, small, hook):
            slots = [lane(f"l_g{tag}{i}") for i in range(4)]
            groups = (tiles + GT - 1) // GT
            mm, added = {}, {}
            last_add = [table]

            offs = {}

            def load(q, n):
                offs[q] = nc.values_load_multi_w_load_instructions(
                    BT[row:row + 1, GT * q:GT * q + n], engines=(mybir.EngineType.DVE,), min_val=0, max_val=top,
                    skip_runtime_bounds_check_because="a node, or a count of bucket starts times 128")[1]

            def add(q, j, table, sums):
                win = table[:, bass.ds(offs[q][j], width)]
                return v.tensor_tensor(win, win, sums, ALU.add)

            def adds(q):
                n = min(GT, tiles - GT * q)
                DVE.do(None, 0, load, q, n)
                DVE.wait(mm[q])
                b = q % 2
                m = prev = last_add[0]
                for j in range(n):
                    col = slice(j * width, (j + 1) * width)
                    DVE.wait(prev)
                    prev = DVE.mark(add, q, j, AGG, PS[b][:, col])
                    if small:
                        at, k = small[0], small[1]
                        DVE.wait(m)
                        m = DVE.mark(add, q, j, BIG[at:at + k, NX:2 * NX], PS[2 + b][at:at + k, col])
                last_add[0] = added[q] = m if small else prev

            DVE.wait(table)
            for q in range(groups):
                n = min(GT, tiles - GT * q)
                sl, b = q % 4, q % 2
                POOL.wait(mm.get(q - 4), idx_ready(q))
                for j in range(n):
                    got = slots[sl].mark(POOL, g.indirect_dma_start,
                        out=G[:, sl, j, :], out_offset=None, in_=rows,
                        in_offset=bass.IndirectOffsetOnAxis(ap=idx(GT * q + j), axis=0))
                DVE.wait(mm.get(q - 4), idx_ready(q))
                for j in range(n):
                    ms = DVE.mark(v.tensor_scalar, S[:, sl, j, 0:width], IOTA[:, 0:width], rel(GT * q + j), None,
                                                  ALU.is_equal)
                if small and small[3]:
                    for j in range(n):
                        ms = DVE.mark(v.tensor_scalar, *small[3](q, j))
                if q:
                    adds(q - 1)
                PE.wait(got, ms, added.get(q - 2))
                for j in range(n):
                    m = PE.mark(t.matmul, PS[b][:, j * width:(j + 1) * width], G[:, sl, j, :],
                                         S[:, sl, j, 0:width], start=True, stop=True)
                    if small:
                        m = PE.mark(t.matmul, PS[2 + b][small[0]:small[0] + small[1], j * width:(j + 1) * width],
                                             small[2](q, j), S[:, sl, j, 0:width], start=True, stop=True)
                mm[q] = m
                if hook:
                    hook(q, added.get(q - 1))
            adds(groups - 1)
            return added[groups - 1], mm[groups - 1]

        def types(f):
            return (32, 9, lambda q, j: OT[q % 4][:, j, :],
                    lambda q, j: (OT[q % 4][:, j, :], IOTA[:, 0:9], f(GT * q + j), None, ALU.is_equal))

        def part1_quick():
            self_loops()
            work = sort(1, SRCi, POSA)
            place = []
            taken = [0]
            l_na = lane("l_qna")
            empty = [None]

            def hook(q, sums):
                if q % 10 == 4 and q // 10 < 32:
                    SP.wait(m_na, sums)
                    empty[0] = empty_rows(l_na, q // 10)
                while taken[0] < (q + 1) * 0.55:
                    got = next(work, 0)
                    if got:
                        place.append(got[0:3])
                    else:
                        taken[0] += 1

            POOL.wait(m_typ)
            agg = aggregate("q0", m_clear, 0, NP, W0, C, x, lambda c: SRCi[:, c:c + 1],
                            lambda c: REL0[:, c:c + 1], lambda q: None, types(lambda c: TYPF[:, c:c + 1]), hook)
            rest_of_part1("q", agg, place, work, empty[0])

        def part1_general():
            l_nb, l_sb, l_rb, l_na = lane("l_nb"), lane("l_sb"), lane("l_rb"), lane("l_gna")
            SP.wait(m_nb, m_na)
            for i in range(4):
                null_b = l_nb.mark(SP, nc.sync.dma_start, RBv[:, 416 * i:416 * (i + 1), :], NULB)
            for i in range(32):
                null_a = empty_rows(l_na, i)
            DVE.done()
            DVE.wait(m_clear)
            m = DVE.mark(v.tensor_scalar, TMPI, DSTi, 127, None, ALU.bitwise_and)
            DVE.mark(v.tensor_copy, RECB[:, :, 0].bitcast(I32), SRCi)
            DVE.wait(m)
            DVE.mark(v.tensor_copy, RECB[:, :, 1], TMPI)
            m_recb = DVE.mark(v.tensor_copy, RECB[:, :, 2], TYPF[:, 0:C])
            POOL.wait(null_b, m_recb)
            for got in sort(0, DSTi, POSB):
                if not got:
                    continue
                k, u, m, table_b = got
                POOL.wait(m)
                for c in range(CW * k, CW * k + u):
                    done_b = l_sb.mark(POOL, g.indirect_dma_start,
                        out=RBd, out_offset=bass.IndirectOffsetOnAxis(ap=POSB[:, c:c + 1], axis=0),
                        in_=RECB[:, c, :], in_offset=None)
            DVE.roll()
            PE.roll()
            place = [got[0:3] for got in sort(1, SRCi, POSA) if got]
            DVE.done()
            PE.done()
            ACE.wait(done_b, m_clear)
            m_types = clear_types()
            self_loops()
            SP.wait(done_b, DVE.last(), PE.last())
            got_rb = l_rb.mark(SP, nc.sync.dma_start, RBs, RBv)
            for q_ in (DVE, PE, POOL):
                q_.roll()
            DVE.wait(table_b)
            agg = aggregate("g0", m_types, 0, (NB - 1) * P, P, NT, x, lambda c: RBs[:, c, 0:1].bitcast(I32),
                            lambda c: RBs[:, c, 1:2], lambda q: got_rb, types(lambda c: RBs[:, c, 2:3]), None)
            rest_of_part1("g", agg, place, iter(()), null_a)

        def rest_of_part1(tag, agg, place_a, work, null_a):
            agg_done, mm_done = agg
            DVE.done()
            PE.done()
            m_eb = weights()
            for q_ in (DVE, PE, POOL, ACE):
                q_.roll()
            l_ea = [lane(f"l_{tag}ea{i}") for i in range(2)]
            l_sa = [lane(f"l_{tag}sa{i}") for i in range(2)]
            scat_a = {}
            DVE.wait(mm_done, null_a)
            DVE.done()
            for i in range(2):
                m_one = DVE.mark(v.memset, RECA[i][:, :, 18:20], 1.0)
            ea_v = ea.rearrange("p (c w) -> p c w", w=16)
            ea_free = {}

            def records(k):
                while len(place_a) <= min(k + 1, NCH - 1):
                    got = next(work)
                    if got:
                        place_a.append(got[0:3])
                _, u, pm = place_a[k]
                i = k % 2
                c0 = CW * k
                SP.wait(ea_free.get(k - 2), null_a)
                m = l_ea[i].mark(SP, nc.sync.dma_start, EAR[i][:, 0:u, :], ea_v[:, c0:c0 + u, :])
                ACE.wait(m, scat_a.get(k - 2), m_rels, m_one)
                ACE.mark(s.copy, RECA[i][:, 0:u, 2:18], EAR[i][:, 0:u, :])
                ACE.mark(s.copy, RECA[i][:, 0:u, 0].bitcast(I32), DSTi[:, c0:c0 + u])
                m = ACE.mark(s.copy, RECA[i][:, 0:u, 1], RELS[:, c0:c0 + u])
                ea_free[k] = m
                POOL.wait(m, pm, null_a)
                for c in range(u):
                    scat_a[k] = l_sa[i].mark(POOL, g.indirect_dma_start,
                        out=RAd, out_offset=bass.IndirectOffsetOnAxis(ap=POSA[:, c0 + c:c0 + c + 1], axis=0),
                        in_=RECA[i][:, c, :], in_offset=None)

            records(0)

            l_xb = [lane(f"l_{tag}xb{i}") for i in range(4)]
            l_x1 = [lane(f"l_{tag}x1{i}") for i in range(2)]
            free_xb, free_xm, free_ps, free_g, store = {}, {}, {}, {}, {}
            xv = x.rearrange("(b p) f -> b p f", p=P)
            x1v = X1d.rearrange("(b p) f -> p b f", p=P)
            SP.wait(agg_done, mm_done)
            DVE.wait(mm_done)
            ACE.wait(agg_done, mm_done)
            PE.wait(agg_done, m_eb)
            rec_next = [1]
            agg_init = None
            tr_free = {}
            for gr in range(NB // GB):
                yb = Y[gr % 2]
                st = ST[gr % 2]
                for bi in range(GB):
                    b = gr * GB + bi
                    sl, s2 = b % 4, b % 2
                    col = slice(b * P, (b + 1) * P)
                    SP.wait(free_xb.get(b - 4))
                    mx = l_xb[sl].mark(SP, nc.sync.dma_start, XB[sl], xv[b])
                    PE.wait(mx, free_ps.get(b - 2))
                    t4 = PS[2 + s2]
                    PE.mark(t.transpose, t4[:, 0:P], XB[sl], IDN[:])
                    PE.mark(t.matmul, t4[:, P:2 * P], WM[:], AGG[:, col], start=True, stop=False)
                    m = PE.mark(t.matmul, t4[:, P:2 * P], EB[32:41, 0, :], T9[:, col], start=False, stop=True)
                    ACE.wait(m, free_xm.get(b - 2))
                    m = ACE.mark(s.copy, XMT[s2], t4[:, 0:2 * P])
                    free_ps[b] = m
                    gb = PS[6 + s2]
                    PE.wait(m, free_g.get(b - 2))
                    PE.mark(t.matmul, gb[:, :], ONE[64:65, :], BR[0:1, 2, :], start=True, stop=False)
                    PE.mark(t.matmul, gb[:, 0:384], XMT[s2][:, P:2 * P], WI[:], start=False, stop=False)
                    PE.mark(t.matmul, gb[:, 0:256], XMT[s2][:, 0:P], WH[:, 0:256], start=False, stop=False)
                    m = PE.mark(t.matmul, gb[:, 384:512], XMT[s2][:, 0:P], WH[:, 256:384], start=False, stop=True)
                    free_xm[b] = m
                    ACE.wait(m, free_g.get(b - 2))
                    mrz = ACE.mark(s.activation, RZ[s2], gb[:, 0:256], ACT.Sigmoid)
                    DVE.wait(mrz)
                    d, e = DD[s2][:, 0:P], DD[s2][:, P:2 * P]
                    m = DVE.mark(v.tensor_tensor, d, RZ[s2][:, 0:P], gb[:, 384:512], ALU.mult)
                    DVE.wait(m)
                    m = DVE.mark(v.tensor_tensor, d, d, gb[:, 256:384], ALU.add)
                    ACE.wait(m)
                    mt = ACE.mark(s.activation, TN[s2], d, ACT.Tanh)
                    DVE.wait(mt)
                    m1 = DVE.mark(v.tensor_tensor, d, XB[sl], TN[s2], ALU.subtract)
                    DVE.mark(v.tensor_tensor, e, XB[sl], TN[s2], ALU.add)
                    DVE.wait(m1)
                    m = DVE.mark(v.tensor_tensor, d, d, RZ[s2][:, P:2 * P], ALU.mult)
                    DVE.wait(m)
                    free_xb[b] = m
                    m = DVE.mark(v.tensor_tensor, yb[:, bi, :], d, e, ALU.add)
                    free_g[b] = m
                    DVE.wait(m)
                    m = DVE.mark(v.bn_stats, st[:, bi, 0:6], yb[:, bi, :])
                    DVE.wait(m)
                    mst = DVE.mark(v.bn_aggr, st[:, bi, 6:8], st[:, bi, 0:6])
                    if b % 3 == 2 and rec_next[0] < NCH:
                        records(rec_next[0])
                        rec_next[0] += 1
                ACE.wait(mst)
                m = ACE.mark(s.activation, st[:, :, 7], st[:, :, 7], ACT.Sqrt, bias=EP[:, 0:1])
                DVE.wait(m)
                m = DVE.mark(v.reciprocal, st[:, :, 7], st[:, :, 7])
                DVE.wait(m)
                for bi in range(GB):
                    m = DVE.mark(v.tensor_scalar, yb[:, bi, :], yb[:, bi, :], st[:, bi, 6:7], st[:, bi, 7:8],
                                                 ALU.subtract, ALU.mult)
                SP.wait(m)
                PE.wait(m)
                store[gr] = l_x1[gr % 2].mark(SP, nc.sync.dma_start, x1v[:, gr * GB:(gr + 1) * GB, :], yb)
                for bi in range(GB):
                    b = gr * GB + bi
                    pt = PS[bi % 2]
                    PE.wait(tr_free.get(b - 2))
                    m = PE.mark(t.transpose, pt[:, 0:P], yb[:, bi, :], IDN[:])
                    ACE.wait(m)
                    agg_init = ACE.mark(s.copy, AGG[:, b * P:(b + 1) * P], pt[:, 0:P])
                    tr_free[b] = agg_init
                DVE.wait(store.get(gr - 1), agg_init)
            while rec_next[0] < NCH:
                records(rec_next[0])
                rec_next[0] += 1


        def part2(tag, tiles, overlap):
            l_ra = [lane(f"l_{tag}ra{i}") for i in range(3)]
            l_ho = [lane(f"l_{tag}ho{i}") for i in range(2)]
            l_xo = [lane(f"l_{tag}xo{i}") for i in range(2)]
            l_out = [lane(f"l_{tag}out{i}") for i in range(2)]
            rows_of = [X1d, H1d, H2d]
            x1v = X1d.rearrange("(b p) f -> p b f", p=P)
            ra_mark, ix_mark, pe_used = {}, {}, {}
            NRC = NTP // RC
            nk = (NP + 511) // 512
            wrote, init = [], None

            def chunk(i):
                SP.wait(pe_used.get(i - 3), ix_mark.get(i - 3))
                m = l_ra[i % 3].mark(SP, nc.sync.dma_start, RAR[i % 3], RAv[:, RC * i:RC * (i + 1), :])
                ra_mark[i] = m
                ACE.wait(m)
                ACE.mark(s.copy, IDXA[:, RC * i:RC * (i + 1)], RAR[i % 3][:, :, 0].bitcast(I32))
                ix_mark[i] = ACE.mark(s.copy, RELA[:, RC * i:RC * (i + 1)], RAR[i % 3][:, :, 1])

            def ready_a(q):
                i = q * GT // RC
                if (q * GT) % RC == 0:
                    if q:
                        pe_used[i - 1] = PE.last()
                    if i + 1 < NRC and i + 1 not in ix_mark:
                        chunk(i + 1)
                return ix_mark[i]

            def layer(lay, wrote, init):
                fin = lay == 2
                hid_f, out_f, ot_f, sto, trs_f, y_f = {}, {}, {}, {}, {}, {}
                hv = None if fin else rows_of[lay + 1].rearrange("(b p) f -> p b f", p=P)

                def dense(k, sums):
                    w = min(512, NP - 512 * k)
                    nb = w // P
                    col = slice(512 * k, 512 * k + w)
                    s2 = k % 2
                    if fin:
                        SP.wait(y_f.get(k - 2))
                        mx = l_xo[s2].mark(SP, nc.sync.dma_start, XO[s2][:, 0:nb, :], x1v[:, 4 * k:4 * k + nb, :])
                    for h in range(2):
                        bank = PS[4 + h]
                        PE.wait(hid_f.get((k - 1, h)), *sums)
                        PE.mark(t.matmul, bank[:, 0:w], W1A[:, lay, h * P:(h + 1) * P], AGG[:, col], start=True,
                                         stop=False)
                        m = PE.mark(t.matmul, bank[:, 0:w], MM[:, lay, h * P:(h + 1) * P], T17[:, col],
                                             start=False, stop=True)
                        ACE.wait(m, out_f.get(k - 2))
                        hid_f[(k, h)] = mh = ACE.mark(s.activation,
                            HID[s2][:, h, 0:w], bank[:, 0:w], ACT.Relu, bias=SCL[:, lay, 2 + h:3 + h],
                            scale=SCL[:, lay, h:h + 1])
                        yield
                    PE.wait(mh, ot_f.get(k - 1))
                    PE.mark(t.matmul, PS[6][:, 0:w], W2[:, lay, 0, :], HID[s2][:, 0, 0:w], start=True, stop=False)
                    m = PE.mark(t.matmul, PS[6][:, 0:w], W2[:, lay, 1, :], HID[s2][:, 1, 0:w], start=False,
                                         stop=True)
                    out_f[k] = m
                    ACE.wait(m, *sums)
                    b2 = PV[:, 11 * lay + 10:11 * lay + 11]
                    m = ACE.mark(s.activation, AGG[:, col], PS[6][:, 0:w], ACT.Identity if fin else ACT.Relu,
                                              bias=b2)
                    ot_f[k] = m
                    yield
                    PE.wait(m, trs_f.get(k - 1))
                    for j in range(nb):
                        m = PE.mark(t.transpose, PS[7][:, j * P:(j + 1) * P],
                                                AGG[:, 512 * k + j * P:512 * k + (j + 1) * P], IDN[:])
                    yield
                    DVE.wait(m, sto.get(k - 2))
                    y = TRS[s2]
                    flat = y[:, 0:nb, :].rearrange("p a b -> p (a b)")
                    if not fin:
                        m = DVE.mark(v.tensor_copy, flat, PS[7][:, 0:w])
                        trs_f[k] = m
                        SP.wait(m)
                        sto[k] = l_ho[s2].mark(SP, nc.sync.dma_start, hv[:, 4 * k:4 * k + nb, :], y[:, 0:nb, :])
                        return
                    st = ST2[s2]
                    DVE.wait(mx)
                    m = DVE.mark(v.tensor_tensor, flat, XO[s2][:, 0:nb, :].rearrange("p a b -> p (a b)"),
                                                 PS[7][:, 0:w], ALU.add)
                    trs_f[k] = y_f[k] = m
                    DVE.wait(m)
                    for j in range(nb):
                        m = DVE.mark(v.bn_stats, st[:, j, 0:6], y[:, j, :])
                    DVE.wait(m)
                    for j in range(nb):
                        m = DVE.mark(v.bn_aggr, st[:, j, 6:8], st[:, j, 0:6])
                    ACE.wait(m)
                    m = ACE.mark(s.activation, st[:, 0:nb, 7], st[:, 0:nb, 7], ACT.Sqrt, bias=EP[:, 0:1])
                    yield
                    DVE.wait(m)
                    m = DVE.mark(v.reciprocal, st[:, 0:nb, 7], st[:, 0:nb, 7])
                    DVE.wait(m)
                    for j in range(nb):
                        m = DVE.mark(v.tensor_scalar, y[:, j, :], y[:, j, :], st[:, j, 6:7], st[:, j, 7:8],
                                                     ALU.subtract, ALU.mult)
                    SP.wait(m)
                    full = min(nb, (N - 512 * k) // P)
                    if full:
                        sto[k] = l_out[s2].mark(SP, nc.sync.dma_start,
                            out[512 * k:512 * k + full * P, :].rearrange("(b p) f -> p b f", p=P),
                            y[:, 0:full, :])
                    rest = min(w, N - 512 * k) - full * P
                    if rest:
                        sto[k] = l_out[s2].mark(SP, nc.sync.dma_start,
                            out[512 * k + full * P:512 * k + full * P + rest, :], y[0:rest, full, :])

                run = [0, None]

                def hook(q, sums):
                    if run[1] is None and run[0] < nk and sums and when(run[0]) <= GT * q:
                        run[1] = dense(run[0], (sums,))
                        run[0] += 1
                    if run[1] is not None and next(run[1], "end") == "end":
                        run[1] = None

                POOL.wait(*wrote)
                DVE.wait(init, *wrote)
                small = None
                if lay == 0:
                    chunk(0)
                    chunk(1)
                    small = (0, 17, lambda q, j: RAR[(q * GT // RC) % 3][:, (q * GT + j) % RC, 2:19], None)
                sums = aggregate(f"{tag}{lay + 1}", None, 32, (NB - 1) * P, P, tiles, rows_of[lay],
                                 lambda c: IDXA[:, c:c + 1], lambda c: RELA[:, c:c + 1],
                                 ready_a if lay == 0 else lambda q: None, small, hook if overlap else None)
                while run[1] is not None and next(run[1], "end") != "end":
                    pass
                for k in range(run[0], nk):
                    for _ in dense(k, sums):
                        pass
                return [sto[nk - 1], sto[nk - 2]], ot_f[nk - 1]

            for lay in range(3):
                wrote, init = layer(lay, wrote, init)
                for q_ in (DVE, PE, POOL, ACE):
                    q_.roll()

        branch(0, m_f1, part1_quick, part1_general)
        m = DVE.mark(v.tensor_tensor, LIM[0:1, :], TEND[0:1, 1, :], LIM[0:1, :], ALU.is_gt)
        DVE.wait(m)
        m = DVE.mark(v.tensor_reduce, FW[0:1, 5:6], LIM[0:1, :], mybir.AxisListType.X, ALU.max)
        DVE.wait(m)
        m = DVE.mark(v.tensor_scalar, FL[0:1, 1:2], FW[0:1, 5:6], 0.5, None, ALU.is_lt)
        branch(1, m, lambda: part2("q", NTF, True), lambda: part2("g", NT, False))


_SHAPE = (12500, 128)


def _layout(i):
    import numpy as np
    rows = NX - N

    def edges(a, fill):
        a = np.concatenate([a, np.full((P * C - E,) + a.shape[1:], fill, a.dtype)])
        return np.swapaxes(a.reshape((C, P) + a.shape[1:]), 0, 1).reshape(P, -1)

    def cols(a):
        return a.reshape(2, P).T

    pv = []
    for k in range(3):
        for n in ("g", "be", "rm", "rv", "b1"):
            pv.append(cols(i[f"L1_gnn_{n}0"] if k == 0 and n != "b1" else i["L1_gnn_b1_0"] if k == 0
                           else i[f"L1_gnn_{n}"][k - 1]))
        pv.append((i["L1_gnn_b2_0"] if k == 0 else i["L1_gnn_b2"][k - 1]).reshape(P, 1))
    enc = [np.concatenate([i["L1_gnn_enc_w0"], i["L1_gnn_enc_b0"][None]])]
    for k in range(2):
        enc.append(np.concatenate([i["L1_gnn_enc_w"][k], i["L1_gnn_enc_b"][k][None]]))
    w1 = i["L1_gnn_w1"]
    w2 = [i["L1_gnn_w2_0"], i["L1_gnn_w2"][0], i["L1_gnn_w2"][1]]
    d = {
        "x": np.concatenate([i["x"], np.zeros((rows, P), i["x"].dtype)]),
        "dst": edges(i["dst"], NP), "src": edges(i["src"], NP), "typ": edges(i["edge_type_9"], 0),
        "ea": edges(i["edge_attr_16"], 0),
        "wmsgT": i["L0_gnn_W_msg"].T, "wihT": i["L0_gnn_W_ih"].T, "whhT": i["L0_gnn_W_hh"].T,
        "emb": i["L0_gnn_edge_embed"], "bmsg": i["L0_gnn_b_msg"][None], "bih": i["L0_gnn_b_ih"][None],
        "bhh": i["L0_gnn_b_hh"][None],
        "encT": np.concatenate([e.T for e in enc], axis=1),
        "w1a": np.concatenate([i["L1_gnn_w1_0"], w1[0, 0:P], w1[1, 0:P]], axis=1),
        "w1b": np.concatenate([w1[0, P:], w1[1, P:]], axis=1),
        "w2": np.concatenate([w[k * P:(k + 1) * P] for w in w2 for k in range(2)], axis=1),
        "pv": np.concatenate(pv, axis=1),
    }
    return {k: np.ascontiguousarray(a) for k, a in d.items()}


def kernel(**inputs):
    import numpy as np
    import concourse.bacc as bacc
    from concourse.bass_utils import run_bass_kernel_spmd

    nc = bacc.Bacc("TRN2", target_bir_lowering=False, num_devices=1)
    arrays, args = {}, []
    for name, a in _layout({k: np.asarray(a) for k, a in inputs.items()}).items():
        arrays[f"in_{name}"] = a
        args.append(nc.dram_tensor(f"in_{name}", a.shape, mybir.dt.from_np(a.dtype), kind="ExternalInput").ap())
    args.append(nc.dram_tensor("out_0", _SHAPE, F32, kind="ExternalOutput").ap())
    program(nc, *args)
    r = run_bass_kernel_spmd(nc, [arrays], core_ids=[0])
    return r.results[0]["out_0"]
```
